# Optimizing a Trainium2 kernel written in Bass

```python
import numpy as np
import jax
import jax.numpy as jnp

def _softmax(x, axis=-1):
    return jax.nn.softmax(x, axis=axis)

def _gelu(x):
    return jax.nn.gelu(x, approximate=True)

def _silu(x):
    return jax.nn.silu(x)

def _sigmoid(x):
    return jax.nn.sigmoid(x)

def _layernorm(x, axis=-1, eps=1e-05):
    m = jnp.mean(x, axis=axis, keepdims=True)
    v = jnp.var(x, axis=axis, keepdims=True)
    return (x - m) / jnp.sqrt(v + eps)

def _scatter_add(tgt, idx, src, axis=0):
    return tgt.at[idx].add(src)

def _segment_sum(src, seg, n):
    return jax.ops.segment_sum(src, seg, n)
kernel_name = 'mk_sandwich_d1_jaxref_r4_d56d23'

def setup_inputs(seed: int=0):
    np.random.seed(seed)
    _w = jnp.asarray

    def _L0_attn_setup():
        import jax, jax.numpy as jnp
        import numpy as np
        D_MODEL = 512
        N_HEADS = 32
        N_KV_HEADS = 8
        HEAD_DIM = D_MODEL // N_HEADS
        ROPE_THETA = 10000.0

        def _build_rope_cache(seq_len, head_dim, theta):
            half = head_dim // 2
            inv_freq = 1.0 / theta ** (jnp.arange(half, dtype=jnp.float32) / half)
            pos = jnp.arange(seq_len, dtype=jnp.float32)
            freqs = jnp.outer(pos, inv_freq)
            return (jnp.cos(freqs), jnp.sin(freqs))

        def _apply_rope(x, cos, sin):
            x_even = x[..., ::2]
            x_odd = x[..., 1::2]
            c = cos[None, None]
            s = sin[None, None]
            rot_even = x_even * c - x_odd * s
            rot_odd = x_even * s + x_odd * c
            return jnp.stack((rot_even, rot_odd), axis=-1).reshape(x.shape)
        key = jax.random.key(seed)
        k0, k1, k2, k3, k4 = jax.random.split(key, 5)
        B, S = (2, 512)
        scale = 0.02
        x = jax.random.normal(k0, (B, S, D_MODEL), dtype=jnp.float32)
        Wq = jax.random.normal(k1, (D_MODEL, N_HEADS * HEAD_DIM), dtype=jnp.float32) * scale
        Wk = jax.random.normal(k2, (D_MODEL, N_KV_HEADS * HEAD_DIM), dtype=jnp.float32) * scale
        Wv = jax.random.normal(k3, (D_MODEL, N_KV_HEADS * HEAD_DIM), dtype=jnp.float32) * scale
        Wo = jax.random.normal(k4, (D_MODEL, D_MODEL), dtype=jnp.float32) * scale
        return {'x': x, 'Wq': Wq, 'Wk': Wk, 'Wv': Wv, 'Wo': Wo}
    _L0_attn_in = _L0_attn_setup()

    def _L0_ffn_setup():
        import jax, jax.numpy as jnp
        import numpy as np
        E = 64
        K = 6
        CAP = 128
        SCALE = 1.0
        H = 512
        I = 192
        SI = I * 2
        B, S = (2, 256)

        def _moe(x, gate_w, gate_up_proj, down_proj, shared_gate_w, shared_up_w, shared_down_w):
            b, s, h = x.shape
            T = b * s
            xf = x.reshape(T, h)
            scores = jax.nn.softmax(xf @ gate_w.T, axis=-1)
            topk_w, topk_idx = jax.lax.top_k(scores, K)
            topk_w = topk_w * SCALE
            flat_e = topk_idx.reshape(-1)
            order = jnp.argsort(flat_e)
            sorted_e = flat_e[order]
            sorted_tok = (order // K).astype(jnp.int32)
            sorted_w = topk_w.reshape(-1)[order]
            counts = jnp.zeros((E,), jnp.int32).at[flat_e].add(1)
            offsets = jnp.cumsum(counts) - counts
            pos = jnp.arange(T * K, dtype=jnp.int32) - offsets[sorted_e]
            buf_tok = jnp.full((E, CAP), T, jnp.int32).at[sorted_e, pos].set(sorted_tok, mode='drop')
            buf_w = jnp.zeros((E, CAP), x.dtype).at[sorted_e, pos].set(sorted_w, mode='drop')
            xp = jnp.concatenate([xf, jnp.zeros((1, h), x.dtype)], axis=0)
            gx = xp[buf_tok]
            gu = jnp.einsum('ech,ehi->eci', gx, gate_up_proj)
            g, u = jnp.split(gu, 2, axis=-1)
            hid = jax.nn.silu(g) * u
            eo = jnp.einsum('eci,eih->ech', hid, down_proj) * buf_w[..., None]
            routed = jnp.zeros((T + 1, h), x.dtype).at[buf_tok.reshape(-1)].add(eo.reshape(-1, h))[:T]
            shared = jax.nn.silu(xf @ shared_gate_w.T) * (xf @ shared_up_w.T) @ shared_down_w.T
            return (routed + shared).reshape(b, s, h)
        key = jax.random.key(seed)
        ks = jax.random.split(key, 7)
        x = jax.random.normal(ks[0], (B, S, H), jnp.float32)
        gate_w = jax.random.normal(ks[1], (E, H), jnp.float32) * 0.02
        gate_up_proj = jax.random.normal(ks[2], (E, H, 2 * I), jnp.float32) * 0.02
        down_proj = jax.random.normal(ks[3], (E, I, H), jnp.float32) * 0.02
        shared_gate_w = jax.random.normal(ks[4], (SI, H), jnp.float32) * 0.02
        shared_up_w = jax.random.normal(ks[5], (SI, H), jnp.float32) * 0.02
        shared_down_w = jax.random.normal(ks[6], (H, SI), jnp.float32) * 0.02
        return dict(x=x, gate_w=gate_w, gate_up_proj=gate_up_proj, down_proj=down_proj, shared_gate_w=shared_gate_w, shared_up_w=shared_up_w, shared_down_w=shared_down_w)
    _L0_ffn_in = _L0_ffn_setup()
    _d = {'L0_attn_x': _L0_attn_in['x'], 'L0_attn_Wq': _L0_attn_in['Wq'], 'L0_attn_Wk': _L0_attn_in['Wk'], 'L0_attn_Wv': _L0_attn_in['Wv'], 'L0_attn_Wo': _L0_attn_in['Wo'], 'L0_ffn_gate_w': _L0_ffn_in['gate_w'], 'L0_ffn_gate_up_proj': _L0_ffn_in['gate_up_proj'], 'L0_ffn_down_proj': _L0_ffn_in['down_proj'], 'L0_ffn_shared_gate_w': _L0_ffn_in['shared_gate_w'], 'L0_ffn_shared_up_w': _L0_ffn_in['shared_up_w'], 'L0_ffn_shared_down_w': _L0_ffn_in['shared_down_w']}
    _x0 = _d['L0_attn_x']
    _d['L0_attn_x'] = jax.random.normal(jax.random.fold_in(jax.random.key(seed), 1), (4, 1024, 512), dtype=_x0.dtype)
    del _x0
    return _d

def reference(L0_attn_x, L0_attn_Wq, L0_attn_Wk, L0_attn_Wv, L0_attn_Wo, L0_ffn_gate_w, L0_ffn_gate_up_proj, L0_ffn_down_proj, L0_ffn_shared_gate_w, L0_ffn_shared_up_w, L0_ffn_shared_down_w):

    def _L0_attn_ref(x, Wq, Wk, Wv, Wo):
        import jax, jax.numpy as jnp
        import numpy as np
        D_MODEL = 512
        N_HEADS = 32
        N_KV_HEADS = 8
        HEAD_DIM = D_MODEL // N_HEADS
        ROPE_THETA = 10000.0

        def _build_rope_cache(seq_len, head_dim, theta):
            half = head_dim // 2
            inv_freq = 1.0 / theta ** (jnp.arange(half, dtype=jnp.float32) / half)
            pos = jnp.arange(seq_len, dtype=jnp.float32)
            freqs = jnp.outer(pos, inv_freq)
            return (jnp.cos(freqs), jnp.sin(freqs))

        def _apply_rope(x, cos, sin):
            x_even = x[..., ::2]
            x_odd = x[..., 1::2]
            c = cos[None, None]
            s = sin[None, None]
            rot_even = x_even * c - x_odd * s
            rot_odd = x_even * s + x_odd * c
            return jnp.stack((rot_even, rot_odd), axis=-1).reshape(x.shape)
        B, S, _ = x.shape
        q = (x @ Wq).reshape(B, S, N_HEADS, HEAD_DIM).transpose(0, 2, 1, 3)
        k = (x @ Wk).reshape(B, S, N_KV_HEADS, HEAD_DIM).transpose(0, 2, 1, 3)
        v = (x @ Wv).reshape(B, S, N_KV_HEADS, HEAD_DIM).transpose(0, 2, 1, 3)
        cos, sin = _build_rope_cache(S, HEAD_DIM, ROPE_THETA)
        q = _apply_rope(q, cos, sin)
        k = _apply_rope(k, cos, sin)
        repeat = N_HEADS // N_KV_HEADS
        if repeat > 1:
            k = jnp.repeat(k, repeat, axis=1)
            v = jnp.repeat(v, repeat, axis=1)
        scores = jnp.einsum('bhqd,bhkd->bhqk', q, k) / jnp.sqrt(jnp.float32(HEAD_DIM))
        causal = jnp.tril(jnp.ones((S, S), dtype=bool))
        neg = -jnp.finfo(scores.dtype).max
        scores = jnp.where(causal[None, None], scores, neg)
        probs = jax.nn.softmax(scores.astype(jnp.float32), axis=-1).astype(x.dtype)
        out = jnp.einsum('bhqk,bhkd->bhqd', probs, v)
        out = out.transpose(0, 2, 1, 3).reshape(B, S, D_MODEL)
        return out @ Wo

    def _L0_ffn_ref(x, gate_w, gate_up_proj, down_proj, shared_gate_w, shared_up_w, shared_down_w):
        import jax, jax.numpy as jnp
        import numpy as np
        E = 64
        K = 6
        CAP = 128
        SCALE = 1.0
        H = 512
        I = 192
        SI = I * 2
        B, S = (2, 256)

        def _moe(x, gate_w, gate_up_proj, down_proj, shared_gate_w, shared_up_w, shared_down_w):
            b, s, h = x.shape
            T = b * s
            xf = x.reshape(T, h)
            scores = jax.nn.softmax(xf @ gate_w.T, axis=-1)
            topk_w, topk_idx = jax.lax.top_k(scores, K)
            topk_w = topk_w * SCALE
            flat_e = topk_idx.reshape(-1)
            order = jnp.argsort(flat_e)
            sorted_e = flat_e[order]
            sorted_tok = (order // K).astype(jnp.int32)
            sorted_w = topk_w.reshape(-1)[order]
            counts = jnp.zeros((E,), jnp.int32).at[flat_e].add(1)
            offsets = jnp.cumsum(counts) - counts
            pos = jnp.arange(T * K, dtype=jnp.int32) - offsets[sorted_e]
            buf_tok = jnp.full((E, CAP), T, jnp.int32).at[sorted_e, pos].set(sorted_tok, mode='drop')
            buf_w = jnp.zeros((E, CAP), x.dtype).at[sorted_e, pos].set(sorted_w, mode='drop')
            xp = jnp.concatenate([xf, jnp.zeros((1, h), x.dtype)], axis=0)
            gx = xp[buf_tok]
            gu = jnp.einsum('ech,ehi->eci', gx, gate_up_proj)
            g, u = jnp.split(gu, 2, axis=-1)
            hid = jax.nn.silu(g) * u
            eo = jnp.einsum('eci,eih->ech', hid, down_proj) * buf_w[..., None]
            routed = jnp.zeros((T + 1, h), x.dtype).at[buf_tok.reshape(-1)].add(eo.reshape(-1, h))[:T]
            shared = jax.nn.silu(xf @ shared_gate_w.T) * (xf @ shared_up_w.T) @ shared_down_w.T
            return (routed + shared).reshape(b, s, h)
        return _moe(x, gate_w, gate_up_proj, down_proj, shared_gate_w, shared_up_w, shared_down_w)
    x = L0_attn_x
    x = x + _layernorm(_L0_attn_ref(_layernorm(x, axis=-1), L0_attn_Wq, L0_attn_Wk, L0_attn_Wv, L0_attn_Wo), axis=-1)
    x = x + _layernorm(_L0_ffn_ref(_layernorm(x, axis=-1), L0_ffn_gate_w, L0_ffn_gate_up_proj, L0_ffn_down_proj, L0_ffn_shared_gate_w, L0_ffn_shared_up_w, L0_ffn_shared_down_w), axis=-1)
    return x

_drawn_inputs = setup_inputs


def setup_inputs(seed=0):
    import zlib

    import numpy as np

    out = dict(_drawn_inputs(seed))
    spreads = {}
    factors = {}
    for name, (base, spread) in spreads.items():
        noise = np.random.default_rng([zlib.crc32(name.encode()), seed]).standard_normal(out[name].shape)
        drawn = base * np.exp(spread * noise) if base else spread * noise
        out[name] = jnp.asarray(drawn.astype(out[name].dtype))
    for name, factor in factors.items():
        out[name] = (out[name] * factor).astype(out[name].dtype)
    return out
```

```python
import numpy as np
import concourse.bass as bass
from concourse import mybir
from contextlib import ExitStack

NB, S, D = 4, 1024, 512
H, KVH, HD = 32, 8, 16
REP = H // KVH
P = 128
TT = S // P
NT = NB * TT
DC = D // P
NROT = H + KVH
NQK = NROT * HD
NQKV = NQK + KVH * HD
E, TOPK, CAP = 64, 6, 128
I, SI = 192, 384
IH = I // 2
SIC = SI // P
ROW = D + E + 1
TOKCOL = D + E
T = NB * S
EPS = 1e-5
NEG = -3.0e38
PIECES = 6
QROWS = PIECES * HD
BROWS = QROWS + 2
HALF = 512
QPH = HALF // P


def score_units():
    first, second = [], []
    for half, out in ((0, first), (1, second)):
        for kh in range(half + 1):
            for q in range(QPH * half, QPH * (half + 1)):
                w = min(HALF, (q + 1) * P - HALF * kh)
                n = {128: 4, 256: 2, 384: 1, 512: 1}[w]
                for h in range(0, REP, n):
                    out.append((half, q, kh, w, tuple(range(h, h + n))))
    return first, second


FIRST, SECOND = score_units()
UNITS = FIRST + SECOND
NU = len(UNITS)
NU0 = len(FIRST)
PUNITS = [(qh, kt, max(0, kt * P - qh * HALF)) for qh in range(2) for kt in range(QPH * (qh + 1))]
NP = len(PUNITS)
HALF1 = QPH
DIAG = [kt * P >= qh * HALF for qh, kt, _ in PUNITS]
NDIAG = sum(DIAG)


def spread():
    cost = [len(u[4]) * (u[3] + (P if u[1] // QPH == u[2] else 0)) for u in UNITS]
    total, work = sum(cost), sum(HALF - c for _, _, c in PUNITS)
    out, done, spent, u = [], 0, 0, 0
    for _, _, c in PUNITS:
        two = []
        for part in range(2):
            done += (HALF - c) / 2
            n = 0
            while u < NU and spent + cost[u] / 2 <= total * done / work + 1:
                spent += cost[u]
                u += 1
                n += 1
            two.append(n)
        out.append(two)
    out[-1][1] += NU - u
    return out


SPREAD = spread()


def program(nc, x, w_qkv, w_o, gate_w, w_gu, w_dn, sh_gu, sh_dn, rope_c, rope_s, out, x1_d, acc_d, disp_d):
    f32, bf16, i32, u32 = mybir.dt.float32, mybir.dt.bfloat16, mybir.dt.int32, mybir.dt.uint32
    ALU, AX, ACT = mybir.AluOpType, mybir.AxisListType.X, mybir.ActivationFunctionType

    ctx = ExitStack()
    with ctx:
        def sb(name, shape, dt, where=ctx):
            return where.enter_context(nc.sbuf_tensor(name, shape, dt))

        def sem(name):
            return ctx.enter_context(nc.semaphore(name))

        id_b = sb("id_b", [P, P], bf16)
        id_f = sb("id_f", [P, P], f32)
        minus_half = sb("minus_half", [P, TT], f32)
        ps = ctx.enter_context(nc.psum_tensor("ps", [P, 8, 512], f32))
        psb = [ps[:, k, :].bitcast(bf16) for k in range(8)]

        att = ExitStack()
        wqkv_sb = sb("wqkv_sb", [P, DC, NQKV], f32, att)
        wo_sb = sb("wo_sb", [P, DC, D], f32, att)
        gw_sb = sb("gw_sb", [P, DC, E], f32, att)
        shgu_sb = sb("shgu_sb", [P, DC, 2 * SI], f32, att)
        shdn_sb = sb("shdn_sb", [P, SIC, D], f32, att)
        ropec_sb = sb("ropec_sb", [P, TT, HD], f32, att)
        ropes_sb = sb("ropes_sb", [P, TT, HD], f32, att)
        causal = sb("causal", [P, P], bf16, att)
        before = sb("before", [P, P], bf16, att)
        ones_b = sb("ones_b", [P, P], bf16, att)
        iota_e = sb("iota_e", [P, E], f32, att)
        blank = sb("blank", [P, ROW], f32, att)
        tok = sb("tok", [P, 1], f32, att)
        qT = sb("qT", [P, 2, H, HALF], bf16, att)
        kT = sb("kT", [P, KVH, S], bf16, att)
        v_all = sb("v_all", [P, TT, KVH, HD], f32, att)
        v_ones = sb("v_ones", [P, TT, 32], f32, att)
        raw = sb("raw", [P, KVH, S], f32, att)
        rmax = sb("rmax", [P, 48], f32, att)
        mb = [sb(f"mb{k}", [P, 32], bf16, att) for k in range(2)]
        mT = [sb(f"mT{k}", [32, P], bf16, att) for k in range(2)]
        taken = sb("taken", [P, E], bf16, att)
        pick = sb("pick", [P, E], bf16, att)
        slot_i = sb("slot_i", [P, 4, TOPK], i32, att)

        wa = ExitStack()
        xin = [sb(f"xin{k}", [P, D], f32, wa) for k in range(2)]
        xn = [sb(f"xn{k}", [P, D], f32, wa) for k in range(2)]
        xT = [sb(f"xT{k}", [P, DC, P], f32, wa) for k in range(2)]
        rot_a = sb("rot_a", [P, NROT, HD], f32, wa)
        rot_b = sb("rot_b", [P, NROT, HD], f32, wa)
        rot = [sb(f"rot{k}", [P, NROT, HD], f32, wa) for k in range(2)]
        rest = sb("rest", [P, NROT, HD], f32, wa)
        stk = [sb(f"stk{k}", [P, NROT, QROWS], bf16, wa) for k in range(2)]
        st6 = sb("st6", [P, 2, 6], f32, wa)
        mv = sb("mv", [P, 2, 2], f32, wa)
        vr = sb("vr", [P, 2], f32, wa)
        rstd = sb("rstd", [P, 2], f32, wa)
        wa.close()
        wa = ExitStack()
        pr = [sb(f"pr{k}", [P, REP, HALF], f32, wa) for k in range(2)]
        wa.close()
        wa = ExitStack()
        xres = [sb(f"xres{k}", [P, D], f32, wa) for k in range(2)]
        rden = sb("rden", [P, H], f32, wa)
        an = [sb(f"an{k}", [P, H, HD], f32, wa) for k in range(2)]
        anT = sb("anT", [P, DC, P], f32, wa)
        un = sb("un", [P, D], f32, wa)
        x1 = [sb(f"x1{k}", [P, D], f32, wa) for k in range(2)]
        x2 = [sb(f"x2{k}", [P, ROW], f32, wa) for k in range(4)]
        x2T = sb("x2T", [P, DC, P], f32, wa)
        sgm = sb("sgm", [P, SI], f32, wa)
        sg1 = sb("sg1", [P, SI], f32, wa)
        hid = sb("hid", [P, SI], f32, wa)
        hidT = sb("hidT", [P, SIC, P], f32, wa)
        ysh = [sb(f"ysh{k}", [P, D], f32, wa) for k in range(2)]
        onehot = sb("onehot", [P, TOPK, E], f32, wa)
        ohpos = sb("ohpos", [P, TOPK, E], f32, wa)
        top8 = sb("top8", [P, 8], f32, wa)
        idx8 = sb("idx8", [P, 8], u32, wa)
        idxf = sb("idxf", [P, TOPK], f32, wa)
        posk = sb("posk", [P, TOPK], f32, wa)
        over = sb("over", [P, TOPK], f32, wa)
        slotf = sb("slotf", [P, TOPK], f32, wa)
        nmax = sb("nmax", [P, 1], f32, wa)
        esum = sb("esum", [P, 1], f32, wa)
        rsum = sb("rsum", [P, 1], f32, wa)
        pexp = sb("pexp", [P, E], f32, wa)
        cst6 = sb("cst6", [P, 2, 6], f32, wa)
        cmv = sb("cmv", [P, 2, 2], f32, wa)
        cvr = sb("cvr", [P, 2], f32, wa)
        crs = sb("crs", [P, 2], f32, wa)
        wa.close()
        att.close()

        ex = ExitStack()
        gu_sb = [sb(f"gu_sb{k}", [P, DC, 2 * I], f32, ex) for k in range(4)]
        dn_sb = [sb(f"dn_sb{k}", [IH, 2, D], f32, ex) for k in range(4)]
        gx = [sb(f"gx{k}", [P, ROW], f32, ex) for k in range(4)]
        gxT = [sb(f"gxT{k}", [P, DC, P], f32, ex) for k in range(2)]
        esg = sb("esg", [P, I], f32, ex)
        es1 = sb("es1", [P, I], f32, ex)
        eh = [sb(f"eh{k}", [P, I], f32, ex) for k in range(2)]
        ehT = [sb(f"ehT{k}", [IH, 2, P], f32, ex) for k in range(2)]
        eo = [sb(f"eo{k}", [P, D], f32, ex) for k in range(2)]
        ex.close()
        fi = ExitStack()
        FT = 4
        fy = [sb(f"fy{k}", [P, FT, D], f32, fi) for k in range(2)]
        fx = [sb(f"fx{k}", [P, FT, D], f32, fi) for k in range(2)]
        fo = [sb(f"fo{k}", [P, FT, D], f32, fi) for k in range(2)]
        fst = sb("fst", [P, 2, FT, 6], f32, fi)
        fmv = sb("fmv", [P, 2, FT, 2], f32, fi)
        fvr = sb("fvr", [P, 2, FT], f32, fi)
        frs = sb("frs", [P, 2, FT], f32, fi)
        fi.close()

        phase_end = sem("phase_end")
        waits_passed = sem("waits_passed")
        const_ready = sem("const_ready")
        weights_in = sem("weights_in")
        disp_blank = sem("disp_blank")
        acc_blank = sem("acc_blank")
        x_in = [sem(f"x_in{k}") for k in range(2)]
        var_ready, rstd_ready, xn_ready = sem("var_ready"), sem("rstd_ready"), sem("xn_ready")
        xt_done, xt_copied = sem("xt_done"), sem("xt_copied")
        qkv_done, qkv_read = sem("qkv_done"), sem("qkv_read")
        high_ready, rest_ready, mid_ready = sem("high_ready"), sem("rest_ready"), sem("mid_ready")
        low_ready, repeats_ready = sem("low_ready"), sem("repeats_ready")
        stack_done, stack_copied = sem("stack_done"), sem("stack_copied")
        sc_done, sc_reduced = sem("sc_done"), sem("sc_reduced")
        max_ready, maxT_done, maxT_copied = sem("max_ready"), sem("maxT_done"), sem("maxT_copied")
        max_rows = [sem(f"max_rows{k}") for k in range(2)]
        st_done, exp_done, masked = sem("st_done"), sem("exp_done"), sem("masked")
        v_ready, pv_done, pv_copied = sem("v_ready"), sem("pv_done"), sem("pv_copied")
        raw_done, an_ready = sem("raw_done"), sem("an_ready")
        t1_done, anT_copied, wo_done = sem("t1_done"), sem("anT_copied"), sem("wo_done")
        xres_in = [sem(f"xres_in{k}") for k in range(2)]
        cvar_ready, crs_ready, un_ready, x1_ready = sem("cvar_ready"), sem("crs_ready"), sem("un_ready"), sem("x1_ready")
        x1_out = [sem(f"x1_out{k}") for k in range(2)]
        x2_ready, x2t_done, x2T_copied = sem("x2_ready"), sem("x2t_done"), sem("x2T_copied")
        rt_done, gu_done, nmax_ready, pexp_ready, sgm_ready = (
            sem("rt_done"), sem("gu_done"), sem("nmax_ready"), sem("pexp_ready"), sem("sgm_ready"))
        pick_ready, pos_done, slot_ready = sem("pick_ready"), sem("pos_done"), sem("slot_ready")
        hid_ready, ht_done, hidT_copied = sem("hid_ready"), sem("ht_done"), sem("hidT_copied")
        dn_done, ysh_ready = sem("dn_done"), sem("ysh_ready")
        ysh_out = [sem(f"ysh_out{k}") for k in range(2)]
        sent = [sem(f"sent{k}") for k in range(4)]
        ew_in = [sem(f"ew_in{k}") for k in range(4)]
        gx_in = [sem(f"gx_in{k}") for k in range(4)]
        gxt_done, gxT_copied = sem("gxt_done"), sem("gxT_copied")
        egu_done, esg_ready, eh_ready = sem("egu_done"), sem("esg_ready"), sem("eh_ready")
        eht_done, ehT_copied, edn_done, eo_ready = sem("eht_done"), sem("ehT_copied"), sem("edn_done"), sem("eo_ready")
        added = [sem(f"added{k}") for k in range(2)]
        f_in = [sem(f"f_in{k}") for k in range(2)]
        fvar_ready, frs_ready, fo_ready = sem("fvar_ready"), sem("frs_ready"), sem("fo_ready")
        f_out = [sem(f"f_out{k}") for k in range(2)]

        block = ctx.enter_context(nc.Block())

        ENGINES, PHASES = 5, 3

        def wait_apart(eng, s, value):
            eng.wait_ge(s, value)
            eng.sem_inc(waits_passed, 1)

        def end_phase(eng, b, phase):
            eng.drain().then_inc(phase_end, 1)
            wait_apart(eng, phase_end, (b * PHASES + phase + 1) * ENGINES)

        def end_late_phase(eng, k):
            eng.drain().then_inc(phase_end, 1)
            eng.wait_ge(phase_end, (NB * PHASES + k + 1) * ENGINES)

        x_t = x.rearrange("(n p) d -> n p d", p=P)
        out_t = out.rearrange("(n p) d -> n p d", p=P)
        x1_t = x1_d.rearrange("(n p) d -> n p d", p=P)
        acc_t = acc_d.rearrange("(n p) d -> n p d", p=P)

        @block.sync
        def _(sp):
            sp.dma_start(ropec_sb[:], rope_c.rearrange("(t p) c -> p t c", p=P)).then_inc(weights_in, 16)
            sp.dma_start(ropes_sb[:], rope_s.rearrange("(t p) c -> p t c", p=P)).then_inc(weights_in, 16)
            sp.dma_start(wqkv_sb[:], w_qkv.rearrange("(c p) n -> p c n", p=P)).then_inc(weights_in, 16)
            sp.dma_start(wo_sb[:], w_o.rearrange("(c p) n -> p c n", p=P)).then_inc(weights_in, 16)
            sp.dma_start(gw_sb[:], gate_w.rearrange("(c p) n -> p c n", p=P)).then_inc(weights_in, 16)
            sp.dma_start(shgu_sb[:], sh_gu.rearrange("(c p) n -> p c n", p=P)).then_inc(weights_in, 16)
            sp.dma_start(shdn_sb[:], sh_dn.rearrange("(c p) n -> p c n", p=P)).then_inc(weights_in, 16)
            with sp.Fori(0, NB) as b:
                for t in range(TT):
                    if t >= 2:
                        sp.wait_ge(xn_ready, TT * b + t - 1)
                    sp.dma_start(xin[t % 2][:], x_t[bass.ds(TT * b + t, 1)].squeeze(0)).then_inc(x_in[t % 2], 16)
                end_phase(sp, b, 0)

                def rows(g, half):
                    gg = KVH * b + g
                    sp.wait_ge(maxT_copied, 2 * gg + half + 1)
                    for part in range(2):
                        sp.dma_start(qT[QROWS + part:QROWS + part + 1, half, bass.ds(REP * g, REP), :],
                                     mT[half][16 * part:16 * part + 16, :]).then_inc(max_rows[half], 16)
                rows(0, 0)
                with sp.Fori(0, KVH - 1) as g:
                    rows(g, 1)
                    rows(g + 1, 0)
                rows(KVH - 1, 1)
                end_phase(sp, b, 1)

                for s in range(TT + 3):
                    if s < TT:
                        if s >= 2:
                            sp.wait_ge(x1_ready, TT * b + s - 1)
                        sp.dma_start(xres[s % 2][:], x_t[bass.ds(TT * b + s, 1)].squeeze(0)).then_inc(xres_in[s % 2], 16)
                    t = s - 1
                    if 0 <= t < TT:
                        sp.wait_ge(x1_ready, TT * b + t + 1)
                        sp.dma_start(x1_t[bass.ds(TT * b + t, 1)].squeeze(0), x1[t % 2][:]).then_inc(x1_out[t % 2], 16)
                    t = s - 3
                    if 0 <= t < TT:
                        sp.wait_ge(ysh_ready, TT * b + t + 1)
                        sp.dma_start(acc_t[bass.ds(TT * b + t, 1)].squeeze(0), ysh[t % 2][:]).then_inc(ysh_out[t % 2], 16)
                for k in range(2):
                    wait_apart(sp, x1_out[k], 16 * (TT // 2) * (b + 1))
                    wait_apart(sp, ysh_out[k], 16 * (TT // 2) * (b + 1))
                end_phase(sp, b, 2)

            def load_expert(e, k):
                sp.dma_start(gu_sb[k][:], w_gu[bass.ds(e, 1)].squeeze(0).rearrange("(c p) n -> p c n", p=P)).then_inc(ew_in[k], 16)
                sp.dma_start(dn_sb[k][:], w_dn[bass.ds(e, 1)].squeeze(0).rearrange("(c p) n -> p c n", p=IH)).then_inc(ew_in[k], 16)
                sp.dma_start(gx[k][:], disp_d[bass.ds(CAP * e, CAP)]).then_inc(gx_in[k], 16)

            for k in range(4):
                load_expert(k, k)
            with sp.Fori(0, E // 4 - 1) as i:
                for k in range(4):
                    sp.wait_ge(edn_done, 4 * i + k + 1)
                    sp.wait_ge(added[k % 2], 16 * (2 * i + k // 2 + 1))
                    load_expert(4 * i + 4 + k, k)
            end_late_phase(sp, 0)
            fin = T // (P * FT)
            acc_f = acc_d[0:T].rearrange("(n f p) d -> n p f d", p=P, f=FT)
            x1_f = x1_d.rearrange("(n f p) d -> n p f d", p=P, f=FT)
            out_f = out.rearrange("(n f p) d -> n p f d", p=P, f=FT)

            def load_f(j, k):
                sp.dma_start(fy[k][:], acc_f[j]).then_inc(f_in[k], 16)
                sp.dma_start(fx[k][:], x1_f[j]).then_inc(f_in[k], 16)

            load_f(0, 0)
            load_f(1, 1)
            for j in range(fin):
                sp.wait_ge(fo_ready, j + 1)
                sp.dma_start(out_f[j], fo[j % 2][:]).then_inc(f_out[j % 2], 16)
                if j + 2 < fin:
                    load_f(j + 2, j % 2)
            for k in range(2):
                sp.wait_ge(f_out[k], 16 * fin // 2)

        @block.tensor
        def _(pe):
            pe.wait_ge(const_ready, 1)
            pe.wait_ge(weights_in, 16 * 7)
            XTB = 6

            def bank2(k):
                return ps[:, 2 * k:2 * k + 2, :].rearrange("p a n -> p (a n)")

            with pe.Fori(0, NB) as b:
                def x_transpose(t):
                    n = TT * b + t
                    pe.wait_ge(xn_ready, n + 1)
                    if t >= 1:
                        pe.wait_ge(xt_copied, n)
                    for c in range(DC):
                        last = pe.transpose(ps[:, XTB, c * P:(c + 1) * P], xn[t % 2][:, c * P:(c + 1) * P], id_f[:])
                    last.then_inc(xt_done, 1)

                def qkv_chunk(t, c):
                    n = TT * b + t
                    acc = bank2(t % 2)
                    if c == 0:
                        pe.wait_ge(xt_copied, n + 1)
                        if t >= 2:
                            pe.wait_ge(qkv_read, n - 1)
                    pe.matmul(acc[:, 0:512], xT[t % 2][:, c, :], wqkv_sb[:, c, 0:512], start=c == 0, stop=c == DC - 1)
                    last = pe.matmul(acc[:, 512:NQKV], xT[t % 2][:, c, :], wqkv_sb[:, c, 512:NQKV],
                                     start=c == 0, stop=c == DC - 1)
                    if c == DC - 1:
                        last.then_inc(qkv_done, 1)

                def stack_transpose(t, j):
                    n = TT * b + t
                    if j == 0:
                        pe.wait_ge(low_ready, n + 1)
                        pe.wait_ge(repeats_ready, n + 1)
                    if 5 * t + j >= 2:
                        pe.wait_ge(stack_copied, 5 * n + j - 1)
                    bank = psb[4 + (5 * t + j) % 2]
                    for h in range(8):
                        last = pe.transpose(bank[0:QROWS, h * P:(h + 1) * P], stk[t % 2][:, 8 * j + h, :], id_b[:])
                    last.then_inc(stack_done, 1)

                x_transpose(0)
                for s in range(TT + 2):
                    for c in range(DC):
                        if s < TT:
                            qkv_chunk(s, c)
                        if s >= 2:
                            stack_transpose(s - 2, c)
                    if s + 1 < TT:
                        x_transpose(s + 1)
                    if s >= 2:
                        stack_transpose(s - 2, 4)
                end_phase(pe, b, 0)

                def score_unit(g, u):
                    half, q, kh, w, heads = UNITS[u]
                    if u >= 2:
                        pe.wait_ge(sc_reduced, NU * (KVH * b + g) + u - 1)
                    for k, h in enumerate(heads):
                        o = ps[:, u % 2, k * w:(k + 1) * w]
                        diag = q // QPH == kh
                        last = pe.matmul(o, qT[0:QROWS, half, bass.ds(REP * g + h, 1), q % QPH * P:(q % QPH + 1) * P].squeeze(1),
                                         kT[0:QROWS, bass.ds(g, 1), kh * HALF:kh * HALF + w].squeeze(1),
                                         start=True, stop=not diag)
                        if diag:
                            last = pe.matmul(o[:, w - P:w], id_b[:], causal[:], start=False, stop=True)
                    last.then_inc(sc_done, 1)

                def max_transpose(g, half):
                    pe.wait_ge(max_ready, 2 * (KVH * b + g) + half + 1)
                    pe.transpose(psb[7][0:32, 0:P], mb[half][:], id_b[:]).then_inc(maxT_done, 1)

                def group(g, with_next):
                    gg = KVH * b + g
                    nxt = 0

                    def scores_of_next(n):
                        nonlocal nxt
                        for _ in range(n if with_next else 0):
                            if nxt < 2:
                                pe.wait_ge(sc_reduced, NU * (gg + 1) + nxt - 1)
                            score_unit(g + 1, nxt)
                            nxt += 1

                    def outputs(i):
                        qh, kt, c0 = PUNITS[i]
                        pe.wait_ge(exp_done, 2 * NP * gg + 2 * i + 2)
                        if DIAG[i]:
                            pe.wait_ge(masked, NDIAG * gg + sum(DIAG[:i + 1]))
                        if i == 0:
                            pe.wait_ge(v_ready, gg + 1)
                            pe.wait_ge(pv_copied, 2 * gg + 1)
                        if i == HALF1:
                            pe.wait_ge(pv_copied, 2 * gg + 2)
                        for h in range(REP):
                            last = pe.matmul(ps[32 * h:32 * h + 32, 6, c0:HALF], v_ones[:, kt, :],
                                             pr[i % 2][:, h, 0:HALF - c0], start=kt == 0,
                                             stop=kt == QPH * (qh + 1) - 1)
                        last.then_inc(pv_done, 1)

                    for i, (qh, kt, c0) in enumerate(PUNITS):
                        for pair in range(2):
                            if i == 0 and pair == 0:
                                pe.wait_ge(max_rows[0], 32 * (gg + 1))
                            if i == HALF1 and pair == 0:
                                pe.wait_ge(max_rows[1], 32 * (gg + 1))
                            if i >= 1:
                                pe.wait_ge(exp_done, 2 * NP * gg + 2 * i + pair - 1)
                            for h in range(2):
                                last = pe.matmul(ps[:, 2 + 2 * pair + h, 0:HALF - c0],
                                                 kT[0:BROWS, bass.ds(g, 1), kt * P:(kt + 1) * P].squeeze(1),
                                                 qT[0:BROWS, qh, bass.ds(REP * g + 2 * pair + h, 1), c0:HALF].squeeze(1),
                                                 start=True, stop=True)
                            last.then_inc(st_done, 1)
                            scores_of_next(SPREAD[i][pair])
                        if i >= 1:
                            outputs(i - 1)
                        if i == 1:
                            max_transpose(g, 1)
                        if i == 6 and with_next:
                            max_transpose(g + 1, 0)
                    outputs(NP - 1)

                for u in range(NU):
                    score_unit(0, u)
                max_transpose(0, 0)
                with pe.Fori(0, KVH - 1) as g:
                    group(g, True)
                group(KVH - 1, False)
                end_phase(pe, b, 1)

                for s in range(TT + 3):
                    t = s - 1
                    if 0 <= t < TT:
                        n = TT * b + t
                        pe.wait_ge(an_ready, n + 1)
                        if t >= 3:
                            pe.wait_ge(hidT_copied, n - 2)
                        elif t >= 1:
                            pe.wait_ge(anT_copied, n)
                        anf = an[t % 2][:].rearrange("p h d -> p (h d)")
                        for c in range(DC):
                            last = pe.transpose(ps[:, 2, c * P:(c + 1) * P], anf[:, c * P:(c + 1) * P], id_f[:])
                        last.then_inc(t1_done, 1)
                    t = s - 2
                    if 0 <= t < TT:
                        n = TT * b + t
                        pe.wait_ge(x2_ready, n + 1)
                        if t >= 1:
                            pe.wait_ge(x2T_copied, n)
                        for c in range(DC):
                            last = pe.transpose(ps[:, 7, c * P:(c + 1) * P], x2[t % 4][:, c * P:(c + 1) * P], id_f[:])
                        last.then_inc(x2t_done, 1)
                    t = s
                    if t < TT:
                        n = TT * b + t
                        if t >= 1:
                            pe.wait_ge(an_ready, n)
                        for g in range(KVH):
                            last = pe.transpose(ps[:, g // 4, (g % 4) * P:(g % 4 + 1) * P],
                                                raw[:, g, t * P:(t + 1) * P], id_f[:])
                        last.then_inc(raw_done, 1)
                    t = s - 3
                    if 0 <= t < TT:
                        pe.wait_ge(pick_ready, TT * b + t + 1)
                        pe.matmul(ps[:, 6, E:2 * E], before[:], pick[:], start=True, stop=False)
                        pe.matmul(ps[:, 6, E:2 * E], ones_b[:], taken[:], start=False, stop=True).then_inc(pos_done, 1)
                    t = s - 1
                    if 0 <= t < TT:
                        n = TT * b + t
                        pe.wait_ge(anT_copied, n + 1)
                        if t >= 3:
                            pe.wait_ge(ysh_ready, n - 2)
                        elif t >= 1:
                            pe.wait_ge(un_ready, n)
                        for c in range(DC):
                            last = pe.matmul(ps[:, 3, :], anT[:, c, :], wo_sb[:, c, :], start=c == 0, stop=c == DC - 1)
                        last.then_inc(wo_done, 1)
                    t = s - 3
                    if 0 <= t < TT:
                        n = TT * b + t
                        pe.wait_ge(hid_ready, n + 1)
                        if t + 2 < TT:
                            pe.wait_ge(anT_copied, n + 3)
                        else:
                            pe.wait_ge(hidT_copied, n)
                        for c in range(SIC):
                            last = pe.transpose(ps[:, 2, c * P:(c + 1) * P], hid[:, c * P:(c + 1) * P], id_f[:])
                        last.then_inc(ht_done, 1)
                    t = s - 2
                    if 0 <= t < TT:
                        n = TT * b + t
                        pe.wait_ge(x2T_copied, n + 1)
                        if t >= 1:
                            pe.wait_ge(slot_ready, n)
                        for c in range(DC):
                            last = pe.matmul(ps[:, 6, 0:E], x2T[:, c, :], gw_sb[:, c, :], start=c == 0, stop=c == DC - 1)
                        last.then_inc(rt_done, 1)
                        if t >= 1:
                            pe.wait_ge(hid_ready, n)
                        gu = bank2(2)
                        for c in range(DC):
                            pe.matmul(gu[:, 0:512], x2T[:, c, :], shgu_sb[:, c, 0:512], start=c == 0, stop=c == DC - 1)
                            last = pe.matmul(gu[:, 512:2 * SI], x2T[:, c, :], shgu_sb[:, c, 512:2 * SI],
                                             start=c == 0, stop=c == DC - 1)
                        last.then_inc(gu_done, 1)
                    t = s - 3
                    if 0 <= t < TT:
                        n = TT * b + t
                        pe.wait_ge(hidT_copied, n + 1)
                        if t + 2 < TT:
                            pe.wait_ge(un_ready, n + 3)
                        else:
                            pe.wait_ge(ysh_ready, n)
                        for c in range(SIC):
                            last = pe.matmul(ps[:, 3, :], hidT[:, c, :], shdn_sb[:, c, :], start=c == 0, stop=c == SIC - 1)
                        last.then_inc(dn_done, 1)
                end_phase(pe, b, 2)

            def expert(i, k, skip_first=False, last_one=False):
                e = 4 * i + k
                gu = ps[:, 1 + k % 2, 0:2 * I]

                def half_gate_up(c0):
                    for c in range(c0, c0 + 2):
                        last = pe.matmul(gu, gxT[k % 2][:, c, :], gu_sb[k][:, c, :], start=c == 0, stop=c == DC - 1)
                    return last

                if not last_one:
                    pe.wait_ge(gx_in[(k + 1) % 4], 16 * (i + 1 + (k + 1) // 4))
                    pe.wait_ge(gxT_copied, e + 1)
                    for c in range(DC):
                        last = pe.transpose(ps[:, 0, c * P:(c + 1) * P], gx[(k + 1) % 4][:, c * P:(c + 1) * P], id_f[:])
                    last.then_inc(gxt_done, 1)
                else:
                    pe.wait_ge(gxT_copied, e + 1)
                pe.wait_ge(ew_in[k], 32 * (i + 1))
                half_gate_up(0)
                if not skip_first:
                    hidden_transpose(e - 1, (k - 1) % 2)
                half_gate_up(2).then_inc(egu_done, 1)
                if not skip_first:
                    down(e - 1, (k - 1) % 4)

            def hidden_transpose(e, k2):
                pe.wait_ge(eh_ready, e + 1)
                for c in range(2):
                    last = pe.transpose(ps[0:IH, 3, c * P:(c + 1) * P], eh[k2][:, c * IH:(c + 1) * IH], id_f[:])
                last.then_inc(eht_done, 1)

            def down(e, k):
                pe.wait_ge(ehT_copied, e + 1)
                if not (isinstance(e, int) and e < 2):
                    pe.wait_ge(eo_ready, e - 1)
                for c in range(2):
                    last = pe.matmul(ps[:, 4 + k % 2, :], ehT[k % 2][:, c, :], dn_sb[k][:, c, :], start=c == 0, stop=c == 1)
                last.then_inc(edn_done, 1)

            pe.wait_ge(gx_in[0], 16)
            for c in range(DC):
                last = pe.transpose(ps[:, 0, c * P:(c + 1) * P], gx[0][:, c * P:(c + 1) * P], id_f[:])
            last.then_inc(gxt_done, 1)
            expert(0, 0, skip_first=True)
            for k in range(1, 4):
                expert(0, k)
            with pe.Fori(1, E // 4 - 1) as i:
                for k in range(4):
                    expert(i, k)
            for k in range(4):
                expert(E // 4 - 1, k, last_one=k == 3)
            hidden_transpose(E - 1, 1)
            down(E - 1, 3)
            end_late_phase(pe, 0)

        @block.scalar
        def _(act):
            act.wait_ge(const_ready, 1)
            act.dma_start(disp_d.rearrange("(e p) c -> p e c", p=P),
                          blank[:].unsqueeze(1).broadcast_to((P, E, ROW))).then_inc(disp_blank, 16)
            act.dma_start(acc_d[T:T + CAP], blank[:, 0:D]).then_inc(acc_blank, 16)
            act.drain().then_inc(pv_copied, 1)
            with act.Fori(0, NB) as b:
                def copy_xT(t):
                    act.wait_ge(xt_done, TT * b + t + 1)
                    act.activation(xT[t % 2][:].rearrange("p c j -> p (c j)"), ps[:, 6, :], ACT.Copy).then_inc(xt_copied, 1)

                def copy_stack(t, j):
                    n = TT * b + t
                    act.wait_ge(stack_done, 5 * n + j + 1)
                    src = psb[4 + (5 * t + j) % 2][0:QROWS, :].rearrange("p (h j) -> p h j", j=P)
                    dst = (qT[0:QROWS, t // QPH, 8 * j:8 * j + 8, t % QPH * P:(t % QPH + 1) * P] if j < 4 else kT[0:QROWS, :, t * P:(t + 1) * P])
                    act.activation(dst, src, ACT.Copy).then_inc(stack_copied, 1)

                def middle(t):
                    act.wait_ge(rest_ready, TT * b + t + 1)
                    act.activation(stk[t % 2][:, :, 4 * HD:5 * HD], rest[:], ACT.Copy).then_inc(mid_ready, 1)

                copy_xT(0)
                for s in range(TT + 2):
                    if s >= 2:
                        copy_stack(s - 2, 0)
                        copy_stack(s - 2, 1)
                    if 1 <= s <= TT:
                        middle(s - 1)
                    if s >= 2:
                        copy_stack(s - 2, 2)
                        copy_stack(s - 2, 3)
                    if s + 1 < TT:
                        copy_xT(s + 1)
                    if s >= 2:
                        copy_stack(s - 2, 4)
                end_phase(act, b, 0)

                def copy_maxT(g, half):
                    gg = KVH * b + g
                    act.wait_ge(maxT_done, 2 * gg + half + 1)
                    act.activation(mT[half][:], psb[7][0:32, 0:P], ACT.Copy).then_inc(maxT_copied, 1)

                def copy_outputs(g, half):
                    gg = KVH * b + g
                    act.wait_ge(pv_done, NP * gg + (HALF1 if half == 0 else NP))
                    act.activation(raw[:, bass.ds(g, 1), half * HALF:(half + 1) * HALF].squeeze(1),
                                   ps[:, 6, :], ACT.Copy).then_inc(pv_copied, 1)

                def group(g, with_next):
                    gg = KVH * b + g
                    for i, (qh, kt, c0) in enumerate(PUNITS):
                        for pair in range(2):
                            act.wait_ge(st_done, 2 * NP * gg + 2 * i + pair + 1)
                            if i >= 2 and pair == 0:
                                act.wait_ge(pv_done, NP * gg + i - 1)
                            act.activation(pr[i % 2][:, 2 * pair:2 * pair + 2, 0:HALF - c0],
                                           ps[:, 2 + 2 * pair:4 + 2 * pair, 0:HALF - c0], ACT.Exp,
                                           scale=HD ** -0.5).then_inc(exp_done, 1)
                        if i == 1:
                            copy_maxT(g, 1)
                        if i == HALF1:
                            copy_outputs(g, 0)
                        if i == 6 and with_next:
                            copy_maxT(g + 1, 0)
                    copy_outputs(g, 1)

                copy_maxT(0, 0)
                with act.Fori(0, KVH - 1) as g:
                    group(g, True)
                group(KVH - 1, False)
                end_phase(act, b, 1)

                for s in range(TT + 3):
                    t = s - 1
                    if 0 <= t < TT:
                        act.wait_ge(t1_done, TT * b + t + 1)
                        if t >= 1:
                            act.wait_ge(wo_done, TT * b + t)
                        act.activation(anT[:].rearrange("p c j -> p (c j)"), ps[:, 2, :], ACT.Copy).then_inc(anT_copied, 1)
                    t = s - 2
                    if 0 <= t < TT:
                        act.wait_ge(x2t_done, TT * b + t + 1)
                        if t >= 1:
                            act.wait_ge(gu_done, TT * b + t)
                        act.activation(x2T[:].rearrange("p c j -> p (c j)"), ps[:, 7, :], ACT.Copy).then_inc(x2T_copied, 1)
                    t = s - 3
                    if 0 <= t < TT:
                        act.wait_ge(ht_done, TT * b + t + 1)
                        if t >= 1:
                            act.wait_ge(dn_done, TT * b + t)
                        act.activation(hidT[:].rearrange("p c j -> p (c j)"), ps[:, 2, 0:SI], ACT.Copy).then_inc(hidT_copied, 1)
                    t = s - 2
                    if 0 <= t < TT:
                        n = TT * b + t
                        act.wait_ge(nmax_ready, n + 1)
                        act.activation(pexp[:], ps[:, 6, 0:E], ACT.Exp, bias=nmax[:], accum_out=esum[:]).then_inc(pexp_ready, 1)
                        act.wait_ge(gu_done, n + 1)
                        if t >= 1:
                            act.wait_ge(hid_ready, n)
                        act.activation(sgm[:], ps[:, 4, 0:SI], ACT.Exp, scale=-1.0).then_inc(sgm_ready, 1)
                    t = s - 3
                    if 0 <= t < TT:
                        n = TT * b + t
                        act.wait_ge(dn_done, n + 1)
                        if t >= 2:
                            act.wait_ge(ysh_out[t % 2], 16 * ((TT // 2) * b + t // 2))
                        act.activation(ysh[t % 2][:], ps[:, 3, :], ACT.Copy).then_inc(ysh_ready, 1)
                end_phase(act, b, 2)

            def copy_rowsT(e, k):
                act.wait_ge(gxt_done, e + 1)
                act.activation(gxT[k % 2][:].rearrange("p c j -> p (c j)"), ps[:, 0, :], ACT.Copy).then_inc(gxT_copied, 1)

            def expert(e, k, skip_first=False, last_one=False):
                if not last_one:
                    copy_rowsT(e + 1, k + 1)
                if not skip_first:
                    hiddenT(e - 1, k - 1)
                act.wait_ge(egu_done, e + 1)
                if not skip_first:
                    act.wait_ge(eh_ready, e)
                act.activation(esg[:], ps[:, 1 + k % 2, 0:I], ACT.Exp, scale=-1.0).then_inc(esg_ready, 1)

            def hiddenT(e, k):
                act.wait_ge(eht_done, e + 1)
                act.activation(ehT[k % 2][:].rearrange("p c j -> p (c j)"), ps[0:IH, 3, 0:2 * P], ACT.Copy).then_inc(ehT_copied, 1)

            copy_rowsT(0, 0)
            expert(0, 0, skip_first=True)
            for k in range(1, 4):
                expert(k, k)
            with act.Fori(1, E // 4 - 1) as i:
                for k in range(4):
                    expert(4 * i + k, k)
            for k in range(4):
                expert(E - 4 + k, k, last_one=k == 3)
            hiddenT(E - 1, 1)
            end_late_phase(act, 0)

        @block.vector
        def _(dve):
            dve.wait_ge(const_ready, 1)
            dve.memset(taken[:], 0.0)
            dve.memset(kT[QROWS:P, :, :], 1.0)
            dve.drain()
            dve.wait_ge(weights_in, 16 * 7)
            with dve.Fori(0, NB) as b:
                def stats(t):
                    n = TT * b + t
                    k = t % 2
                    dve.wait_ge(x_in[k], 16 * ((TT // 2) * b + t // 2 + 1))
                    dve.bn_stats(st6[:, k, :], xin[k][:])
                    dve.drain()
                    dve.bn_aggr(mv[:, k, :], st6[:, k, :])
                    dve.drain()
                    dve.tensor_scalar(vr[:, k:k + 1], mv[:, k, 1:2], EPS, None, ALU.add).then_inc(var_ready, 1)

                def normalise(t):
                    n = TT * b + t
                    k = t % 2
                    dve.wait_ge(rstd_ready, n + 1)
                    if t >= 2:
                        dve.wait_ge(xt_done, n - 1)
                    dve.tensor_scalar(xn[k][:], xin[k][:], mv[:, k, 0:1], rstd[:, k:k + 1],
                                      ALU.subtract, ALU.mult).then_inc(xn_ready, 1)

                def rotate(t):
                    n = TT * b + t
                    k = t % 2
                    dve.wait_ge(qkv_done, n + 1)
                    acc = ps[:, 2 * k:2 * k + 2, :].rearrange("p a n -> p (a n)")
                    qk = acc[:, 0:NQK].rearrange("p (h d) -> p h d", d=HD)
                    qk2 = acc[:, 0:NQK].rearrange("p (h d two) -> p h d two", d=HD // 2, two=2)
                    cos = ropec_sb[:, t, :].unsqueeze(1).broadcast_to((P, NROT, HD))
                    sn = ropes_sb[:, t, 0:HD // 2].unsqueeze(1).broadcast_to((P, NROT, HD // 2))
                    sp_ = ropes_sb[:, t, HD // 2:HD].unsqueeze(1).broadcast_to((P, NROT, HD // 2))
                    rb2 = rot_b[:].rearrange("p h (d two) -> p h d two", two=2)
                    dve.tensor_tensor(rot_a[:], qk, cos, ALU.mult)
                    dve.tensor_tensor(rb2[:, :, :, 0], qk2[:, :, :, 1], sn, ALU.mult)
                    dve.tensor_tensor(rb2[:, :, :, 1], qk2[:, :, :, 0], sp_, ALU.mult)
                    dve.tensor_copy(v_all[:, t, :, :], acc[:, NQK:NQKV].rearrange("p (h d) -> p h d", d=HD)).then_inc(qkv_read, 1)
                    dve.drain()
                    if t >= 2:
                        dve.wait_ge(low_ready, n - 1)
                        dve.wait_ge(stack_done, 5 * (n - 1))
                    dve.tensor_tensor(rot[k][:], rot_a[:], rot_b[:], ALU.add)
                    dve.drain()
                    dve.tensor_copy(stk[k][:, :, 0:HD], rot[k][:]).then_inc(high_ready, 1)
                    dve.drain()
                    first = stk[k][:, 0:H, 0:HD]
                    dve.tensor_copy(stk[k][:, 0:H, HD:2 * HD], first)
                    dve.tensor_copy(stk[k][:, 0:H, 2 * HD:3 * HD], first)
                    firstk = stk[k][:, H:NROT, 0:HD]
                    dve.tensor_copy(stk[k][:, H:NROT, 3 * HD:4 * HD], firstk)
                    dve.tensor_copy(stk[k][:, H:NROT, 5 * HD:6 * HD], firstk)

                def repeat_middle(t):
                    n = TT * b + t
                    k = t % 2
                    dve.wait_ge(mid_ready, n + 1)
                    dve.tensor_copy(stk[k][:, 0:H, 3 * HD:4 * HD], stk[k][:, 0:H, 4 * HD:5 * HD])
                    dve.tensor_copy(stk[k][:, H:NROT, HD:2 * HD], stk[k][:, H:NROT, 4 * HD:5 * HD]).then_inc(repeats_ready, 1)

                stats(0)
                stats(1)
                normalise(0)
                for s in range(TT + 1):
                    if s + 1 < TT:
                        normalise(s + 1)
                    if s >= 1:
                        rotate(s - 1)
                    if s + 2 < TT:
                        stats(s + 2)
                    if s >= 1:
                        repeat_middle(s - 1)
                end_phase(dve, b, 0)

                def reduce_unit(g, u):
                    half, q, kh, w, heads = UNITS[u]
                    dve.wait_ge(sc_done, NU * (KVH * b + g) + u + 1)
                    n = len(heads)
                    base = 16 * (half + kh)
                    dst = rmax[:, base:base + 16].rearrange("p (h q) -> p h q", q=QPH)
                    dve.tensor_reduce(dst[:, heads[0]:heads[0] + n, q % QPH],
                                      ps[:, u % 2, 0:n * w].rearrange("p (h k) -> p h k", k=w),
                                      AX, ALU.max).then_inc(sc_reduced, 1)

                def finish_half(g, half):
                    gg = KVH * b + g
                    dve.drain()
                    m = rmax[:, 16 * half:16 * half + 16]
                    if half == 1:
                        dve.tensor_tensor(m, m, rmax[:, 32:48], ALU.max)
                        dve.drain()
                    if not isinstance(g, int):
                        dve.wait_ge(maxT_done, 2 * gg + half - 1)
                    dve.tensor_scalar(mb[half][:, 0:16], m, -1.0, None, ALU.mult)
                    dve.drain()
                    dve.scalar_tensor_tensor(mb[half][:, 16:32], m, -1.0, mb[half][:, 0:16],
                                             ALU.mult, ALU.subtract).then_inc(max_ready, 1)

                def maxima(g):
                    for u in range(NU):
                        reduce_unit(g, u)
                        if u == NU0 - 1:
                            finish_half(g, 0)
                    finish_half(g, 1)

                maxima(0)
                with dve.Fori(0, KVH - 1) as g:
                    maxima(g + 1)
                end_phase(dve, b, 1)

                def layer_stats(src, t, j, inc):
                    dve.bn_stats(cst6[:, j, :], src)
                    dve.drain()
                    dve.bn_aggr(cmv[:, j, :], cst6[:, j, :])
                    dve.drain()
                    dve.tensor_scalar(cvr[:, j:j + 1], cmv[:, j, 1:2], EPS, None, ALU.add).then_inc(inc, 1)

                for s in range(TT + 3):
                    t = s
                    if t < TT:
                        n = TT * b + t
                        dve.wait_ge(raw_done, n + 1)
                        rows = ps[:, 0:2, :].rearrange("p a (h d) -> p (a h) d", d=32)
                        dve.reciprocal(rden[:], rows[:, :, HD])
                        dve.drain()
                        if t >= 2:
                            dve.wait_ge(t1_done, n - 1)
                        dve.tensor_tensor(an[t % 2][:], rows[:, :, 0:HD],
                                          rden[:].unsqueeze(2).broadcast_to((P, H, HD)), ALU.mult).then_inc(an_ready, 1)
                    t = s - 3
                    if 0 <= t < TT:
                        n = TT * b + t
                        dve.wait_ge(pos_done, n + 1)
                        dve.tensor_tensor(ohpos[:], onehot[:], ps[:, 6, E:2 * E].unsqueeze(1).broadcast_to((P, TOPK, E)), ALU.mult)
                        dve.tensor_tensor(taken[:], taken[:], pick[:], ALU.add)
                        dve.drain()
                        dve.tensor_reduce(posk[:], ohpos[:], AX, ALU.add)
                        dve.drain()
                        dve.tensor_scalar(over[:], posk[:], float(CAP), float(E * CAP), ALU.is_ge, ALU.mult)
                        dve.scalar_tensor_tensor(slotf[:], idxf[:], float(CAP), posk[:], ALU.mult, ALU.add)
                        dve.drain()
                        dve.tensor_tensor(slot_i[:, t % 4, :], slotf[:], over[:], ALU.add).then_inc(slot_ready, 1)
                    t = s - 1
                    if 0 <= t < TT:
                        n = TT * b + t
                        dve.wait_ge(wo_done, n + 1)
                        layer_stats(ps[:, 3, :], t, 0, cvar_ready)
                        dve.wait_ge(crs_ready, 2 * n + 1)
                        if t >= 1:
                            dve.wait_ge(x1_ready, n)
                        dve.tensor_scalar(un[:], ps[:, 3, :], cmv[:, 0, 0:1], crs[:, 0:1],
                                          ALU.subtract, ALU.mult).then_inc(un_ready, 1)
                    t = s - 2
                    if 0 <= t < TT:
                        n = TT * b + t
                        dve.wait_ge(rt_done, n + 1)
                        if t >= 1:
                            dve.wait_ge(pexp_ready, n)
                        dve.tensor_reduce(nmax[:], ps[:, 6, 0:E], AX, ALU.max, negate=True).then_inc(nmax_ready, 1)
                    t = s - 1
                    if 0 <= t < TT:
                        n = TT * b + t
                        dve.wait_ge(x1_ready, n + 1)
                        layer_stats(x1[t % 2][:], t, 1, cvar_ready)
                    t = s - 2
                    if 0 <= t < TT:
                        n = TT * b + t
                        sc = x2[t % 4][:, D:D + E]
                        dve.wait_ge(pexp_ready, n + 1)
                        dve.reciprocal(rsum[:], esum[:])
                        dve.drain()
                        dve.tensor_scalar(sc, pexp[:], rsum[:], None, ALU.mult)
                        dve.drain()
                        dve.max(top8[:], sc)
                        dve.drain()
                        dve.max_index(idx8[:], top8[:], sc)
                        dve.drain()
                        dve.tensor_copy(idxf[:], idx8[:, 0:TOPK])
                        dve.drain()
                        dve.tensor_tensor(onehot[:], iota_e[:].unsqueeze(1).broadcast_to((P, TOPK, E)),
                                          idxf[:].unsqueeze(2).broadcast_to((P, TOPK, E)), ALU.is_equal)
                        dve.drain()
                        with nc.allow_low_precision("a sum of zeros and at most one 1"):
                            dve.tensor_reduce(pick[:], onehot[:].rearrange("p k e -> p e k"), AX, ALU.add).then_inc(pick_ready, 1)
                    t = s - 1
                    if 0 <= t < TT:
                        n = TT * b + t
                        dve.wait_ge(crs_ready, 2 * n + 2)
                        if t >= 4:
                            dve.wait_ge(sent[t % 4], 16 * TOPK * ((TT // 4) * b + t // 4))
                        dve.tensor_copy(x2[t % 4][:, TOKCOL:TOKCOL + 1].bitcast(i32), tok[:])
                        dve.tensor_scalar(x2[t % 4][:, 0:D], x1[t % 2][:], cmv[:, 1, 0:1], crs[:, 1:2],
                                          ALU.subtract, ALU.mult).then_inc(x2_ready, 1)
                        dve.tensor_scalar(tok[:], tok[:], float(P), None, ALU.add)
                    t = s - 2
                    if 0 <= t < TT:
                        n = TT * b + t
                        dve.wait_ge(sgm_ready, n + 1)
                        gu = ps[:, 4:6, :].rearrange("p a n -> p (a n)")
                        dve.tensor_scalar(sg1[:], sgm[:], 1.0, None, ALU.add)
                        dve.drain()
                        dve.reciprocal(sgm[:], sg1[:])
                        dve.drain()
                        dve.tensor_tensor(sg1[:], gu[:, 0:SI], sgm[:], ALU.mult)
                        dve.drain()
                        if t >= 1:
                            dve.wait_ge(ht_done, n)
                        dve.tensor_tensor(hid[:], gu[:, SI:2 * SI], sg1[:], ALU.mult).then_inc(hid_ready, 1)
                end_phase(dve, b, 2)

            def gated(e, k):
                dve.wait_ge(esg_ready, e + 1)
                gu = ps[:, 1 + k % 2, :]
                dve.tensor_scalar(es1[:], esg[:], 1.0, None, ALU.add)
                dve.drain()
                dve.reciprocal(esg[:], es1[:])
                dve.drain()
                dve.tensor_tensor(es1[:], gu[:, 0:I], esg[:], ALU.mult)
                dve.drain()
                dve.tensor_tensor(eh[k % 2][:], gu[:, I:2 * I], es1[:], ALU.mult).then_inc(eh_ready, 1)

            def scaled_at(i, k, first=False):
                e = 4 * i + k
                dve.wait_ge(edn_done, e + 1)
                if not first:
                    dve.wait_ge(added[k % 2], 16 * (2 * i + k // 2))
                dve.tensor_scalar(eo[k % 2][:], ps[:, 4 + k % 2, :], gx[k][:, bass.ds(D + e, 1)], None,
                                  ALU.mult).then_inc(eo_ready, 1)

            gated(0, 0)
            for k in range(1, 4):
                gated(k, k)
                scaled_at(0, k - 1, first=k < 3)
            with dve.Fori(1, E // 4) as i:
                for k in range(4):
                    gated(4 * i + k, k)
                    if k == 0:
                        scaled_at(i - 1, 3)
                    else:
                        scaled_at(i, k - 1)
            scaled_at(E // 4 - 1, 3)
            end_late_phase(dve, 0)

            fin = T // (P * FT)

            def f_stats(j):
                k = j % 2
                dve.wait_ge(f_in[k], 32 * (j // 2 + 1))
                for f in range(FT):
                    dve.bn_stats(fst[:, k, f, :], fy[k][:, f, :])
                dve.drain()
                for f in range(FT):
                    dve.bn_aggr(fmv[:, k, f, :], fst[:, k, f, :])
                dve.drain()
                dve.tensor_scalar(fvr[:, k, :], fmv[:, k, :, 1], EPS, None, ALU.add).then_inc(fvar_ready, 1)

            f_stats(0)
            for j in range(fin):
                k = j % 2
                if j + 1 < fin:
                    f_stats(j + 1)
                dve.wait_ge(frs_ready, j + 1)
                if j >= 2:
                    dve.wait_ge(f_out[k], 16 * (j // 2))
                for f in range(FT):
                    dve.tensor_scalar(fy[k][:, f, :], fy[k][:, f, :], fmv[:, k, f, 0:1], frs[:, k, f:f + 1],
                                      ALU.subtract, ALU.mult)
                dve.drain()
                dve.tensor_tensor(fo[k][:], fy[k][:], fx[k][:], ALU.add).then_inc(fo_ready, 1)

        @block.gpsimd
        def _(pool):
            for m in (id_b, id_f):
                pool.memset(m[:], 0.0)
            pool.memset(minus_half[:], -0.5)
            pool.memset(causal[:], 0.0)
            pool.memset(before[:], 0.0)
            pool.memset(ones_b[:], 1.0)
            pool.memset(v_ones[:], 1.0)
            pool.memset(blank[:], 0.0)
            pool.iota(tok[:], pattern=[[0, 1]], base=0, channel_multiplier=1, allow_small_or_imprecise_dtypes=True)
            pool.iota(iota_e[:], pattern=[[1, E]], base=0, channel_multiplier=0, allow_small_or_imprecise_dtypes=True)
            pool.drain()
            for m in (id_b, id_f):
                pool.affine_select(out=m[:], in_=m[:], compare_op=ALU.not_equal, fill=1.0, base=0,
                                   pattern=[[-1, P]], channel_multiplier=1)
            pool.affine_select(out=causal[:], in_=causal[:], compare_op=ALU.is_ge, fill=NEG, base=0,
                               pattern=[[-1, P]], channel_multiplier=1)
            pool.affine_select(out=before[:], in_=before[:], compare_op=ALU.is_ge, fill=1.0, base=0,
                               pattern=[[-1, P]], channel_multiplier=1)
            pool.iota(blank[:, TOKCOL:TOKCOL + 1].bitcast(i32), pattern=[[0, 1]], base=T, channel_multiplier=1)
            pool.drain().then_inc(const_ready, 1)
            with pool.Fori(0, NB) as b:
                def power(t):
                    n = TT * b + t
                    k = t % 2
                    pool.wait_ge(var_ready, n + 1)
                    pool.tensor_tensor(rstd[:, k:k + 1], vr[:, k:k + 1], minus_half[:, 0:1], ALU.pow).then_inc(rstd_ready, 1)

                def pieces(t):
                    n = TT * b + t
                    k = t % 2
                    pool.wait_ge(high_ready, n + 1)
                    if t >= 1:
                        pool.wait_ge(low_ready, n)
                    pool.tensor_tensor(rest[:], rot[k][:], stk[k][:, :, 0:HD], ALU.subtract).then_inc(rest_ready, 1)
                    pool.wait_ge(mid_ready, n + 1)
                    pool.tensor_tensor(stk[k][:, 0:H, 5 * HD:6 * HD], rest[:, 0:H, :], stk[k][:, 0:H, 4 * HD:5 * HD], ALU.subtract)
                    pool.tensor_tensor(stk[k][:, H:NROT, 2 * HD:3 * HD], rest[:, H:NROT, :],
                                       stk[k][:, H:NROT, 4 * HD:5 * HD], ALU.subtract).then_inc(low_ready, 1)

                power(0)
                power(1)
                for s in range(TT + 1):
                    if s >= 1:
                        pieces(s - 1)
                    if s + 2 < TT:
                        power(s + 2)
                end_phase(pool, b, 0)

                def copy_v(g):
                    pool.tensor_copy(v_ones[:, :, 0:HD], v_all[:, :, bass.ds(g, 1), :].squeeze(2)).then_inc(v_ready, 1)

                def group(g, with_next):
                    gg = KVH * b + g
                    d = 0
                    for i, (qh, kt, c0) in enumerate(PUNITS):
                        if DIAG[i]:
                            wait_apart(pool, exp_done, 2 * NP * gg + 2 * i + 2)
                            tile = pr[i % 2][:, :, 0:P]
                            pool.affine_select(out=tile, in_=tile, compare_op=ALU.is_ge, fill=0.0, base=0,
                                               pattern=[[0, REP], [1, P]], channel_multiplier=-1).then_inc(masked, 1)
                            d += 1
                    if with_next:
                        wait_apart(pool, pv_done, NP * (gg + 1))
                        copy_v(g + 1)

                copy_v(0)
                with pool.Fori(0, KVH - 1) as g:
                    group(g, True)
                group(KVH - 1, False)
                end_phase(pool, b, 1)

                pool.wait_ge(disp_blank, 16)
                pool.wait_ge(acc_blank, 16)
                for s in range(TT + 3):
                    t = s - 1
                    if 0 <= t < TT:
                        n = TT * b + t
                        k = t % 2
                        pool.wait_ge(cvar_ready, 2 * n + 1)
                        pool.tensor_tensor(crs[:, 0:1], cvr[:, 0:1], minus_half[:, 0:1], ALU.pow).then_inc(crs_ready, 1)
                        pool.wait_ge(un_ready, n + 1)
                        pool.wait_ge(xres_in[k], 16 * ((TT // 2) * b + t // 2 + 1))
                        if t >= 2:
                            pool.wait_ge(x1_out[k], 16 * ((TT // 2) * b + t // 2))
                            pool.wait_ge(x2_ready, n - 1)
                        pool.tensor_tensor(x1[k][:], un[:], xres[k][:], ALU.add).then_inc(x1_ready, 1)
                        pool.wait_ge(cvar_ready, 2 * n + 2)
                        pool.tensor_tensor(crs[:, 1:2], cvr[:, 1:2], minus_half[:, 0:1], ALU.pow).then_inc(crs_ready, 1)
                    t = s - 3
                    if 0 <= t < TT:
                        n = TT * b + t
                        wait_apart(pool, slot_ready, n + 1)
                        for k in range(TOPK):
                            pool.indirect_dma_start(
                                out=disp_d, out_offset=bass.IndirectOffsetOnAxis(ap=slot_i[:, t % 4, k:k + 1], axis=0),
                                in_=x2[t % 4][:], in_offset=None, bounds_check=E * CAP - 1,
                                oob_is_err=False).then_inc(sent[t % 4], 16)
                for k in range(4):
                    wait_apart(pool, sent[k], 16 * TOPK * (TT // 4) * (b + 1))
                end_phase(pool, b, 2)

            def add_rows(e, k):
                wait_apart(pool, eo_ready, e + 1)
                pool.indirect_dma_start(
                    out=acc_d, out_offset=bass.IndirectOffsetOnAxis(ap=gx[k][:, TOKCOL:TOKCOL + 1].bitcast(i32), axis=0),
                    in_=eo[k % 2][:], in_offset=None, bounds_check=T + CAP - 1, compute_op=ALU.add).then_inc(added[k % 2], 16)

            for k in range(4):
                if k:
                    pool.wait_ge(added[(k - 1) % 2], 16 * ((k - 1) // 2 + 1))
                add_rows(k, k)
            with pool.Fori(1, E // 4) as i:
                for k in range(4):
                    pool.wait_ge(added[(k - 1) % 2], 16 * (2 * i + (k + 1) // 2) if k else 32 * i)
                    add_rows(4 * i + k, k)
            for k in range(2):
                pool.wait_ge(added[k], 16 * E // 2)
            end_late_phase(pool, 0)
            for j in range(T // (P * FT)):
                k = j % 2
                pool.wait_ge(fvar_ready, j + 1)
                pool.tensor_tensor(frs[:, k, :], fvr[:, k, :], minus_half[:, 0:FT], ALU.pow).then_inc(frs_ready, 1)


def rope_tables():
    half = HD // 2
    inv = (np.float32(1) / np.float32(10000) ** (np.arange(half, dtype=np.float32) / np.float32(half))).astype(np.float32)
    ang = np.outer(np.arange(S, dtype=np.float32), inv)
    c, s = np.cos(ang), np.sin(ang)
    return np.repeat(c, 2, axis=1).astype(np.float32), np.concatenate([-s, s], axis=1).astype(np.float32)


def kernel(**inputs):
    import concourse.bacc as bacc
    from concourse.bass_utils import run_bass_kernel_spmd as run

    a = {k: np.asarray(v) for k, v in inputs.items()}
    c, s = rope_tables()
    arrays = {
        "x": a["L0_attn_x"].reshape(T, D),
        "w_qkv": np.concatenate([a["L0_attn_Wq"], a["L0_attn_Wk"], a["L0_attn_Wv"]], axis=1),
        "w_o": a["L0_attn_Wo"],
        "gate_w": np.ascontiguousarray(a["L0_ffn_gate_w"].T),
        "w_gu": a["L0_ffn_gate_up_proj"],
        "w_dn": a["L0_ffn_down_proj"],
        "sh_gu": np.ascontiguousarray(np.concatenate([a["L0_ffn_shared_gate_w"], a["L0_ffn_shared_up_w"]], axis=0).T),
        "sh_dn": np.ascontiguousarray(a["L0_ffn_shared_down_w"].T),
        "rope_c": c,
        "rope_s": s,
    }
    f32 = mybir.dt.float32
    nc = bacc.Bacc("TRN2", target_bir_lowering=False, num_devices=1)
    args = [nc.dram_tensor(f"{k}_dram", v.shape, f32, kind="ExternalInput").ap() for k, v in arrays.items()]
    out = nc.dram_tensor("out_dram", (T, D), f32, kind="ExternalOutput").ap()
    x1_d = nc.dram_tensor("x1_scratch", (T, D), f32, kind="Internal").ap()
    acc_d = nc.dram_tensor("acc_scratch", (T + CAP, D), f32, kind="Internal").ap()
    disp_d = nc.dram_tensor("dispatch_scratch", (E * CAP, ROW), f32, kind="Internal").ap()
    program(nc, *args, out, x1_d, acc_d, disp_d)
    r = run(nc, [{f"{k}_dram": v for k, v in arrays.items()}], core_ids=[0])
    return r.results[0]["out_dram"].reshape(NB, S, D)
```

```python
import numpy as np
import concourse.bass as bass
from concourse import mybir
from contextlib import ExitStack

NB, S, D = 4, 1024, 512
H, KVH, HD = 32, 8, 16
REP = H // KVH
P = 128
TT = S // P
NT = NB * TT
DC = D // P
NROT = H + KVH
NQK = NROT * HD
NQKV = NQK + KVH * HD
E, TOPK, CAP = 64, 6, 128
I, SI = 192, 384
IH = I // 2
SIC = SI // P
ROW = D + E + 1
TOKCOL = D + E
T = NB * S
EPS = 1e-5
NEG = -3.0e38
PIECES = 6
QROWS = PIECES * HD
BROWS = QROWS + 2
HALF = 512
QPH = HALF // P


def score_units():
    first, second = [], []
    for half, out in ((0, first), (1, second)):
        for kh in range(half + 1):
            for q in range(QPH * half, QPH * (half + 1)):
                w = min(HALF, (q + 1) * P - HALF * kh)
                n = {128: 4, 256: 2, 384: 1, 512: 1}[w]
                for h in range(0, REP, n):
                    out.append((half, q, kh, w, tuple(range(h, h + n))))
    return first, second


FIRST, SECOND = score_units()
UNITS = FIRST + SECOND
NU = len(UNITS)
NU0 = len(FIRST)
PUNITS = [(qh, kt, max(0, kt * P - qh * HALF)) for qh in range(2) for kt in range(QPH * (qh + 1))]
NP = len(PUNITS)
HALF1 = QPH
DIAG = [kt * P >= qh * HALF for qh, kt, _ in PUNITS]
NDIAG = sum(DIAG)
SLOTS = 4
LAG = 2


TAIL = 2


def spread():
    cost = [len(u[4]) * (u[3] + (P if u[1] // QPH == u[2] else 0)) for u in UNITS]
    total, work = sum(cost[:NU - TAIL]), sum(HALF - c + P for _, _, c in PUNITS)
    out, done, spent, u = [], 0, 0, 0
    for _, _, c in PUNITS:
        two = []
        for part in range(2):
            done += (HALF - c + P) / 2
            n = 0
            while u < NU - TAIL and spent + cost[u] / 2 <= total * done / work + 1:
                spent += cost[u]
                u += 1
                n += 1
            two.append(n)
        out.append(two)
    out[-1][1] += NU - TAIL - u
    return out


SPREAD = spread()
T1_STEP = 1
T0_UNIT = NU0 + 7
ORDER = list(range(NU))
ORDER.insert(T0_UNIT, "first")
ORDER.insert(sum(map(sum, SPREAD[:T1_STEP + 1])), "second")
T0_STEP = next(i for i in range(NP) if sum(map(sum, SPREAD[:i + 1])) >= T0_UNIT)
BANKS = (0, 1, 7)
BANK_OF = {item: BANKS[k % 3] for k, item in enumerate(ORDER)}
EARLY = sorted(range(NU), key=lambda u: UNITS[u][1])
EARLY_STEP = {u: min(UNITS[u][1] + 4, TT + 1) for u in EARLY}
LATE_Q = 6
EARLY_BANK = {}
for _k, _u in enumerate(EARLY):
    EARLY_BANK[_u] = 7 if UNITS[_u][1] < LATE_Q else BANKS[_k % 3]


def program(nc, x, w_qkv, w_o, gate_w, w_gu, w_dn, sh_gu, sh_dn, rope_c, rope_s, out, x1_d, acc_d, acc2_d, disp_d):
    f32, bf16, i32, u32 = mybir.dt.float32, mybir.dt.bfloat16, mybir.dt.int32, mybir.dt.uint32
    ALU, AX, ACT = mybir.AluOpType, mybir.AxisListType.X, mybir.ActivationFunctionType

    ctx = ExitStack()
    with ctx:
        def sb(name, shape, dt, where=ctx):
            return where.enter_context(nc.sbuf_tensor(name, shape, dt))

        def sem(name):
            return ctx.enter_context(nc.semaphore(name))

        id_b = sb("id_b", [P, P], bf16)
        id_f = sb("id_f", [P, P], f32)
        minus_half = sb("minus_half", [P, TT], f32)
        ps = ctx.enter_context(nc.psum_tensor("ps", [P, 8, 512], f32))
        psb = [ps[:, k, :].bitcast(bf16) for k in range(8)]

        att = ExitStack()
        wqkv_sb = sb("wqkv_sb", [P, DC, NQKV], f32, att)
        wo_sb = sb("wo_sb", [P, DC, D], f32, att)
        gw_sb = sb("gw_sb", [P, DC, E], f32, att)
        shgu_sb = sb("shgu_sb", [P, DC, 2 * SI], f32, att)
        shdn_sb = sb("shdn_sb", [P, SIC, D], f32, att)
        ropec_sb = sb("ropec_sb", [P, TT, HD], f32, att)
        ropes_sb = sb("ropes_sb", [P, TT, HD], f32, att)
        causal = sb("causal", [P, P], bf16, att)
        before = sb("before", [P, P], bf16, att)
        ones_b = sb("ones_b", [P, P], bf16, att)
        iota_e = sb("iota_e", [P, E], f32, att)
        blank = sb("blank", [P, ROW], f32, att)
        tok = sb("tok", [P, 1], f32, att)
        kT = sb("kT", [P, KVH, S], bf16, att)
        v_all = sb("v_all", [P, TT, KVH, HD], f32, att)
        v_ones = sb("v_ones", [P, TT, 32], f32, att)
        raw = sb("raw", [P, KVH, S], f32, att)
        rmax = sb("rmax", [P, 48], f32, att)
        mb = [sb(f"mb{k}", [P, 32], bf16, att) for k in range(2)]
        mT = [sb(f"mT{k}", [32, P], bf16, att) for k in range(2)]
        taken = sb("taken", [P, E], bf16, att)
        pick = sb("pick", [P, E], bf16, att)
        slot_i = sb("slot_i", [P, 4, TOPK], i32, att)

        xin = [sb(f"xin{k}", [P, D], f32, att) for k in range(2)]
        xn = [sb(f"xn{k}", [P, D], f32, att) for k in range(2)]
        st6 = sb("st6", [P, 2, 6], f32, att)
        mv = sb("mv", [P, 2, 2], f32, att)
        vr = sb("vr", [P, 2], f32, att)
        rstd = sb("rstd", [P, 2], f32, att)

        qa = ExitStack()
        qT = sb("qT", [P, 2, H, HALF], bf16, qa)
        wa = ExitStack()
        xT = [sb(f"xT{k}", [P, DC, P], f32, wa) for k in range(2)]
        rot_a = sb("rot_a", [P, NROT, HD], f32, wa)
        rot_b = sb("rot_b", [P, NROT, HD], f32, wa)
        rot = [sb(f"rot{k}", [P, NROT, HD], f32, wa) for k in range(2)]
        rest = sb("rest", [P, NROT, HD], f32, wa)
        stk = [sb(f"stk{k}", [P, NROT, QROWS], bf16, wa) for k in range(2)]
        wa.close()
        wa = ExitStack()
        pr = [sb(f"pr{k}", [P, REP, HALF], f32, wa) for k in range(SLOTS)]
        wa.close()
        qa.close()
        wa = ExitStack()
        xres = [sb(f"xres{k}", [P, D], f32, wa) for k in range(2)]
        rden = sb("rden", [P, H], f32, wa)
        an = [sb(f"an{k}", [P, H, HD], f32, wa) for k in range(2)]
        anT = sb("anT", [P, DC, P], f32, wa)
        un = sb("un", [P, D], f32, wa)
        x1 = [sb(f"x1{k}", [P, D], f32, wa) for k in range(2)]
        x2 = [sb(f"x2{k}", [P, ROW], f32, wa) for k in range(4)]
        x2T = sb("x2T", [P, DC, P], f32, wa)
        sgm = sb("sgm", [P, SI], f32, wa)
        hid = sb("hid", [P, SI], f32, wa)
        hidT = sb("hidT", [P, SIC, P], f32, wa)
        ysh = [sb(f"ysh{k}", [P, D], f32, wa) for k in range(2)]
        onehot = sb("onehot", [P, TOPK, E], f32, wa)
        ohpos = sb("ohpos", [P, TOPK, E], f32, wa)
        top8 = sb("top8", [P, 8], f32, wa)
        idx8 = sb("idx8", [P, 8], u32, wa)
        idxf = sb("idxf", [P, TOPK], f32, wa)
        posk = sb("posk", [P, TOPK], f32, wa)
        over = sb("over", [P, TOPK], f32, wa)
        slotf = sb("slotf", [P, TOPK], f32, wa)
        nmax = sb("nmax", [P, 1], f32, wa)
        esum = sb("esum", [P, 1], f32, wa)
        rsum = sb("rsum", [P, 1], f32, wa)
        pexp = sb("pexp", [P, E], f32, wa)
        cst6 = sb("cst6", [P, 2, 6], f32, wa)
        cmv = sb("cmv", [P, 2, 2], f32, wa)
        cvr = sb("cvr", [P, 2], f32, wa)
        crs = sb("crs", [P, 2], f32, wa)
        wa.close()
        att.close()

        last = ExitStack()
        x1_all = sb("x1_all", [P, NT, D], f32, last)
        ex = ExitStack()
        gu_sb = [sb(f"gu_sb{k}", [P, DC, 2 * I], f32, ex) for k in range(4)]
        dn_sb = [sb(f"dn_sb{k}", [IH, 2, D], f32, ex) for k in range(4)]
        gx = [sb(f"gx{k}", [P, ROW], f32, ex) for k in range(4)]
        gxT = [sb(f"gxT{k}", [P, DC, P], f32, ex) for k in range(2)]
        esg = sb("esg", [P, I], f32, ex)
        eh = [sb(f"eh{k}", [P, I], f32, ex) for k in range(2)]
        ehT = [sb(f"ehT{k}", [IH, 2, P], f32, ex) for k in range(2)]
        eo = [sb(f"eo{k}", [P, D], f32, ex) for k in range(4)]
        etok = [sb(f"etok{k}", [P, 1], i32, ex) for k in range(4)]
        XT = NT // (E // 4)
        ex.close()
        fi = ExitStack()
        FT = 2
        FB = 6
        fy = [sb(f"fy{k}", [P, FT, D], f32, fi) for k in range(FB)]
        fz = [sb(f"fz{k}", [P, FT, D], f32, fi) for k in range(FB)]
        fst = sb("fst", [P, 2, FT, 6], f32, fi)
        fmv = sb("fmv", [P, 2, FT, 2], f32, fi)
        fvr = sb("fvr", [P, 2, FT], f32, fi)
        frs = sb("frs", [P, 2, FT], f32, fi)
        fi.close()
        last.close()

        phase_end = sem("phase_end")
        waits_passed = sem("waits_passed")
        const_ready = sem("const_ready")
        weights_in = sem("weights_in")
        late_weights_in = sem("late_weights_in")
        disp_blank = sem("disp_blank")
        acc_blank = sem("acc_blank")
        x_in = [sem(f"x_in{k}") for k in range(2)]
        var_ready, rstd_ready, xn_ready = sem("var_ready"), sem("rstd_ready"), sem("xn_ready")
        xt_done, xt_copied = sem("xt_done"), sem("xt_copied")
        qkv_done, qkv_read = sem("qkv_done"), sem("qkv_read")
        high_ready, rest_ready, mid_ready = sem("high_ready"), sem("rest_ready"), sem("mid_ready")
        low_ready, repeats_ready = sem("low_ready"), sem("repeats_ready")
        stack_done, stack_copied = sem("stack_done"), sem("stack_copied")
        sc_done, sc_reduced = sem("sc_done"), sem("sc_reduced")
        max_ready, maxT_done, maxT_copied = sem("max_ready"), sem("maxT_done"), sem("maxT_copied")
        max_rows = [sem(f"max_rows{k}") for k in range(2)]
        st_done, exp_done, masked = sem("st_done"), sem("exp_done"), sem("masked")
        v_ready, pv_done, pv_copied = sem("v_ready"), sem("pv_done"), sem("pv_copied")
        raw_done, an_ready = sem("raw_done"), sem("an_ready")
        t1_done, anT_copied, wo_done = sem("t1_done"), sem("anT_copied"), sem("wo_done")
        xres_in = [sem(f"xres_in{k}") for k in range(2)]
        cvar_ready, crs_ready, un_ready, x1_ready = sem("cvar_ready"), sem("crs_ready"), sem("un_ready"), sem("x1_ready")
        x1_out = [sem(f"x1_out{k}") for k in range(2)]
        x2_ready, x2t_done, x2T_copied = sem("x2_ready"), sem("x2t_done"), sem("x2T_copied")
        rt_done, gu_done, nmax_ready, pexp_ready, sgm_ready = (
            sem("rt_done"), sem("gu_done"), sem("nmax_ready"), sem("pexp_ready"), sem("sgm_ready"))
        pick_ready, pos_done, slot_ready = sem("pick_ready"), sem("pos_done"), sem("slot_ready")
        hid_ready, ht_done, hidT_copied = sem("hid_ready"), sem("ht_done"), sem("hidT_copied")
        dn_done, ysh_ready = sem("dn_done"), sem("ysh_ready")
        ysh_out = [sem(f"ysh_out{k}") for k in range(2)]
        rows_sent = sem("rows_sent")
        sent = [sem(f"sent{k}") for k in range(4)]
        ew_in = [sem(f"ew_in{k}") for k in range(4)]
        gx_in = [sem(f"gx_in{k}") for k in range(4)]
        gxt_done, gxT_copied = sem("gxt_done"), sem("gxT_copied")
        egu_done, esg_ready, eh_ready = sem("egu_done"), sem("esg_ready"), sem("eh_ready")
        eht_done, ehT_copied, edn_done, eo_ready = sem("eht_done"), sem("ehT_copied"), sem("edn_done"), sem("eo_ready")
        added = [sem(f"added{k}") for k in range(2)]
        x1_back = sem("x1_back")
        f_in = [sem(f"f_in{k}") for k in range(FB)]
        fvar_ready, frs_ready, fn_ready, fo_ready = sem("fvar_ready"), sem("frs_ready"), sem("fn_ready"), sem("fo_ready")
        f_out = [sem(f"f_out{k}") for k in range(FB)]

        block = ctx.enter_context(nc.Block())

        ENGINES, PHASES = 5, 3

        def wait_apart(eng, s, value):
            eng.wait_ge(s, value)
            eng.sem_inc(waits_passed, 1)

        def end_phase(eng, b, phase):
            eng.drain().then_inc(phase_end, 1)
            wait_apart(eng, phase_end, (b * PHASES + phase + 1) * ENGINES)

        def end_late_phase(eng, k):
            eng.drain().then_inc(phase_end, 1)
            eng.wait_ge(phase_end, (NB * PHASES + k + 1) * ENGINES)

        x_t = x.rearrange("(n p) d -> n p d", p=P)
        out_t = out.rearrange("(n p) d -> n p d", p=P)
        x1_t = x1_d.rearrange("(n p) d -> n p d", p=P)
        acc_t = acc_d.rearrange("(n p) d -> n p d", p=P)
        acc2_t = acc2_d.rearrange("(n p) d -> n p d", p=P)

        @block.sync
        def _(sp):
            for k in range(2):
                sp.dma_start(xin[k][:], x_t[k]).then_inc(x_in[k], 16)
            sp.dma_start(ropec_sb[:], rope_c.rearrange("(t p) c -> p t c", p=P)).then_inc(weights_in, 16)
            sp.dma_start(ropes_sb[:], rope_s.rearrange("(t p) c -> p t c", p=P)).then_inc(weights_in, 16)
            sp.dma_start(wqkv_sb[:], w_qkv.rearrange("(c p) n -> p c n", p=P)).then_inc(weights_in, 16)

            def load_x(b, t):
                sp.dma_start(xin[t % 2][:], x_t[bass.ds(TT * b + t, 1)].squeeze(0)).then_inc(x_in[t % 2], 16)

            with sp.Fori(0, NB) as b:
                for t in range(2, TT):
                    sp.wait_ge(xn_ready, TT * b + t - 1)
                    load_x(b, t)

                def rows(g, half):
                    gg = KVH * b + g
                    sp.wait_ge(maxT_copied, 2 * gg + half + 1)
                    for part in range(2):
                        sp.dma_start(qT[QROWS + part:QROWS + part + 1, half, bass.ds(REP * g, REP), :],
                                     mT[half][16 * part:16 * part + 16, :]).then_inc(max_rows[half], 16)
                rows(0, 0)
                end_phase(sp, b, 0)

                blank_rows = disp_d.rearrange("(g e p) c -> g p e c", g=KVH, p=P)

                def clear(g):
                    sp.dma_start(acc2_t[bass.ds(TT * b + g, 1)].squeeze(0), blank[:, 0:D]).then_inc(acc_blank, 16)
                    with sp.If(b < 1):
                        sp.dma_start(blank_rows[bass.ds(g, 1)].squeeze(0),
                                     blank[:].unsqueeze(1).broadcast_to((P, E // KVH, ROW))).then_inc(disp_blank, 16)

                sp.wait_ge(const_ready, 1)
                with sp.Fori(0, KVH - 1) as g:
                    rows(g, 1)
                    clear(g)
                    rows(g + 1, 0)
                rows(KVH - 1, 1)
                clear(KVH - 1)
                end_phase(sp, b, 1)

                with sp.If(b < NB - 1):
                    following = nc.s_assert_within(b + 1, 0, NB - 1, skip_runtime_bounds_check_because="b < NB - 1 here")
                    for t in range(2):
                        load_x(following, t)
                for s in range(TT + 3):
                    if s < TT:
                        if s >= 2:
                            sp.wait_ge(x1_ready, TT * b + s - 1)
                        sp.dma_start(xres[s % 2][:], x_t[bass.ds(TT * b + s, 1)].squeeze(0)).then_inc(xres_in[s % 2], 16)
                    t = s - 1
                    if 0 <= t < TT:
                        sp.wait_ge(x1_ready, TT * b + t + 1)
                        sp.dma_start(x1_t[bass.ds(TT * b + t, 1)].squeeze(0), x1[t % 2][:]).then_inc(x1_out[t % 2], 16)
                    t = s - 3
                    if 0 <= t < TT:
                        sp.wait_ge(ysh_ready, TT * b + t + 1)
                        sp.dma_start(acc_t[bass.ds(TT * b + t, 1)].squeeze(0), ysh[t % 2][:]).then_inc(ysh_out[t % 2], 16)
                end_phase(sp, b, 2)
            for k in range(2):
                sp.wait_ge(x1_out[k], 16 * (TT // 2 * NB + 1))
                sp.wait_ge(ysh_out[k], 16 * (TT // 2 * NB + 1))
            end_late_phase(sp, 0)

            def load_weights(e, k):
                sp.dma_start(gu_sb[k][:], w_gu[bass.ds(e, 1)].squeeze(0).rearrange("(c p) n -> p c n", p=P)).then_inc(ew_in[k], 16)
                sp.dma_start(dn_sb[k][:], w_dn[bass.ds(e, 1)].squeeze(0).rearrange("(c p) n -> p c n", p=IH)).then_inc(ew_in[k], 16)

            def load_rows(e, k):
                sp.dma_start(gx[k][:], disp_d[bass.ds(CAP * e, CAP)]).then_inc(gx_in[k], 16)

            def load_x1(i):
                sp.dma_start(x1_all[:, bass.ds(XT * i, XT), :],
                             x1_t[bass.ds(XT * i, XT)].rearrange("n p d -> p n d")).then_inc(x1_back, 16)

            for k in range(4):
                load_rows(k, k)
                load_weights(k, k)
            with sp.Fori(0, E // 4 - 1) as i:
                for k in range(4):
                    sp.wait_ge(eo_ready, 4 * i + k + 1)
                    load_rows(4 * i + 4 + k, k)
                    load_weights(4 * i + 4 + k, k)
                load_x1(i)
            load_x1(E // 4 - 1)
            sp.wait_ge(x1_back, 16 * E // 4)
            end_late_phase(sp, 1)
            fin = T // (P * FT)
            acc_f = acc_d[0:T].rearrange("(n f p) d -> n p f d", p=P, f=FT)
            acc2_f = acc2_d[0:T].rearrange("(n f p) d -> n p f d", p=P, f=FT)
            out_f = out.rearrange("(n f p) d -> n p f d", p=P, f=FT)

            def load_f(j, k):
                sp.dma_start(fy[k][:], acc_f[j]).then_inc(f_in[k], 16)
                sp.dma_start(fz[k][:], acc2_f[j]).then_inc(f_in[k], 16)

            for j in range(FB):
                load_f(j, j)
            for j in range(fin):
                sp.wait_ge(fo_ready, j + 1)
                sp.dma_start(out_f[j], fz[j % FB][:]).then_inc(f_out[j % FB], 16)
                if j >= 1 and j - 1 + FB < fin:
                    sp.wait_ge(f_out[(j - 1) % FB], 16 * ((j - 1) // FB + 1))
                    load_f(j - 1 + FB, (j - 1) % FB)
            for k in range(FB):
                sp.wait_ge(f_out[k], 16 * ((fin - 1 - k) // FB + 1))

        @block.tensor
        def _(pe):
            pe.wait_ge(const_ready, 1)
            pe.wait_ge(weights_in, 16 * 3)
            XTB = 6

            def bank2(k):
                return ps[:, 2 * k:2 * k + 2, :].rearrange("p a n -> p (a n)")

            with pe.Fori(0, NB) as b:
                def x_transpose(t):
                    n = TT * b + t
                    pe.wait_ge(xn_ready, n + 1)
                    if t >= 1:
                        pe.wait_ge(xt_copied, n)
                    for c in range(DC):
                        last = pe.transpose(ps[:, XTB, c * P:(c + 1) * P], xn[t % 2][:, c * P:(c + 1) * P], id_f[:])
                    last.then_inc(xt_done, 1)

                def qkv_chunk(t, c):
                    n = TT * b + t
                    acc = bank2(t % 2)
                    if c == 0:
                        pe.wait_ge(xt_copied, n + 1)
                        if t >= 2:
                            pe.wait_ge(qkv_read, n - 1)
                    pe.matmul(acc[:, 0:512], xT[t % 2][:, c, :], wqkv_sb[:, c, 0:512], start=c == 0, stop=c == DC - 1)
                    last = pe.matmul(acc[:, 512:NQKV], xT[t % 2][:, c, :], wqkv_sb[:, c, 512:NQKV],
                                     start=c == 0, stop=c == DC - 1)
                    if c == DC - 1:
                        last.then_inc(qkv_done, 1)

                def stack_transpose(t, j):
                    n = TT * b + t
                    if j == 0:
                        pe.wait_ge(low_ready, n + 1)
                        pe.wait_ge(repeats_ready, n + 1)
                    if 5 * t + j >= 2:
                        pe.wait_ge(stack_copied, 5 * n + j - 1)
                    bank = psb[4 + (5 * t + j) % 2]
                    for h in range(8):
                        last = pe.transpose(bank[0:QROWS, h * P:(h + 1) * P], stk[t % 2][:, 8 * j + h, :], id_b[:])
                    last.then_inc(stack_done, 1)

                def score_unit(g, u, bank):
                    half, q, kh, w, heads = UNITS[u]
                    for k, h in enumerate(heads):
                        o = ps[:, bank, k * w:(k + 1) * w]
                        diag = q // QPH == kh
                        last = pe.matmul(o, qT[0:QROWS, half, bass.ds(REP * g + h, 1), q % QPH * P:(q % QPH + 1) * P].squeeze(1),
                                         kT[0:QROWS, bass.ds(g, 1), kh * HALF:kh * HALF + w].squeeze(1),
                                         start=True, stop=not diag)
                        if diag:
                            last = pe.matmul(o[:, w - P:w], id_b[:], causal[:], start=False, stop=True)
                    last.then_inc(sc_done, 1)

                def early_unit(k):
                    u = EARLY[k]
                    q, bank = UNITS[u][1], EARLY_BANK[u]
                    if k == 0 or UNITS[EARLY[k - 1]][1] != q:
                        pe.wait_ge(stack_copied, 5 * (TT * b + q + 1))
                    before_it = [j for j in range(k) if EARLY_BANK[EARLY[j]] == bank]
                    if bank == 7 and EARLY_STEP[u] > TT and EARLY_STEP[EARLY[before_it[-1]]] <= TT:
                        pe.wait_ge(maxT_copied, 2 * KVH * b + 1)
                    elif before_it:
                        pe.wait_ge(sc_reduced, NU * KVH * b + before_it[-1] + 1)
                    elif bank < 2:
                        pe.wait_ge(qkv_read, TT * b + TT - 1)
                    score_unit(0, u, bank)

                x_transpose(0)
                for s in range(TT + 2):
                    if s == TT + 1:
                        pe.wait_ge(max_ready, 2 * KVH * b + 1)
                        pe.wait_ge(sc_reduced, NU * KVH * b + sum(EARLY_STEP[u] <= TT for u in EARLY))
                        pe.transpose(psb[7][0:32, 0:P], mb[0][:], id_b[:]).then_inc(maxT_done, 1)
                    early = [k for k in range(NU) if EARLY_STEP[EARLY[k]] == s]
                    for c in range(DC):
                        if s < TT:
                            qkv_chunk(s, c)
                        if s >= 2:
                            stack_transpose(s - 2, c)
                        if early and c >= 1:
                            early_unit(early.pop(0))
                    if s + 1 < TT:
                        x_transpose(s + 1)
                    if s >= 2:
                        stack_transpose(s - 2, 4)
                    for k in early:
                        early_unit(k)
                end_phase(pe, b, 0)

                def max_transpose(g, half, bank):
                    pe.wait_ge(max_ready, 2 * (KVH * b + g) + half + 1)
                    pe.transpose(psb[bank][0:32, 0:P], mb[half][:], id_b[:]).then_inc(maxT_done, 1)

                def group(g, with_next):
                    gg = KVH * b + g
                    order = list(ORDER) if with_next else []
                    owner = {}

                    def scores_of_next(n):
                        while order and (n > 0 or order[0] in ("first", "second")):
                            item = order.pop(0)
                            bank = BANK_OF[item]
                            if bank not in owner:
                                pe.wait_ge(sc_reduced, NU * (gg + 1))
                            elif owner[bank] == "second":
                                pe.wait_ge(maxT_copied, 2 * gg + 2)
                            elif owner[bank] == "first":
                                pe.wait_ge(maxT_copied, 2 * gg + 3)
                            else:
                                pe.wait_ge(sc_reduced, NU * (gg + 1) + owner[bank] + 1)
                            owner[bank] = item
                            if item == "first":
                                max_transpose(g + 1, 0, bank)
                            elif item == "second":
                                max_transpose(g, 1, bank)
                            else:
                                score_unit(g + 1, item, bank)
                                n -= 1

                    def outputs(i):
                        qh, kt, c0 = PUNITS[i]
                        pe.wait_ge(exp_done, 2 * NP * gg + 2 * i + 2)
                        if DIAG[i]:
                            pe.wait_ge(masked, NDIAG * gg + sum(DIAG[:i + 1]))
                        if i == 0:
                            pe.wait_ge(v_ready, gg + 1)
                            pe.wait_ge(pv_copied, 2 * gg + 1)
                        if i == HALF1:
                            pe.wait_ge(pv_copied, 2 * gg + 2)
                        for h in range(REP):
                            last = pe.matmul(ps[32 * h:32 * h + 32, 6, c0:HALF], v_ones[:, kt, :],
                                             pr[i % SLOTS][:, h, 0:HALF - c0], start=kt == 0,
                                             stop=kt == QPH * (qh + 1) - 1)
                        last.then_inc(pv_done, 1)

                    for i, (qh, kt, c0) in enumerate(PUNITS):
                        for pair in range(2):
                            if i == 0 and pair == 0:
                                pe.wait_ge(max_rows[0], 32 * (gg + 1))
                            if i == HALF1 and pair == 0:
                                pe.wait_ge(max_rows[1], 32 * (gg + 1))
                            if i >= 1:
                                pe.wait_ge(exp_done, 2 * NP * gg + 2 * i + pair - 1)
                            for h in range(2):
                                last = pe.matmul(ps[:, 2 + 2 * pair + h, 0:HALF - c0],
                                                 kT[0:BROWS, bass.ds(g, 1), kt * P:(kt + 1) * P].squeeze(1),
                                                 qT[0:BROWS, qh, bass.ds(REP * g + 2 * pair + h, 1), c0:HALF].squeeze(1),
                                                 start=True, stop=True)
                            last.then_inc(st_done, 1)
                            scores_of_next(SPREAD[i][pair])
                        if i == T1_STEP and not with_next:
                            pe.wait_ge(sc_reduced, NU * (gg + 1))
                            max_transpose(g, 1, BANK_OF["second"])
                        if i >= LAG:
                            outputs(i - LAG)
                    for k in range(LAG - 1):
                        outputs(NP - LAG + k)
                    scores_of_next(TAIL)
                    outputs(NP - 1)

                with pe.Fori(0, KVH - 1) as g:
                    group(g, True)
                group(KVH - 1, False)
                end_phase(pe, b, 1)
                pe.wait_ge(late_weights_in, 16 * 4)

                for s in range(TT + 3):
                    t = s - 1
                    if 0 <= t < TT:
                        n = TT * b + t
                        pe.wait_ge(an_ready, n + 1)
                        if t >= 3:
                            pe.wait_ge(hidT_copied, n - 2)
                        elif t >= 1:
                            pe.wait_ge(anT_copied, n)
                        anf = an[t % 2][:].rearrange("p h d -> p (h d)")
                        for c in range(DC):
                            last = pe.transpose(ps[:, 2, c * P:(c + 1) * P], anf[:, c * P:(c + 1) * P], id_f[:])
                        last.then_inc(t1_done, 1)
                    t = s - 2
                    if 0 <= t < TT:
                        n = TT * b + t
                        pe.wait_ge(x2_ready, n + 1)
                        if t >= 1:
                            pe.wait_ge(x2T_copied, n)
                        for c in range(DC):
                            last = pe.transpose(ps[:, 7, c * P:(c + 1) * P], x2[t % 4][:, c * P:(c + 1) * P], id_f[:])
                        last.then_inc(x2t_done, 1)
                    t = s
                    if t < TT:
                        n = TT * b + t
                        if t >= 1:
                            pe.wait_ge(an_ready, n)
                        for g in range(KVH):
                            last = pe.transpose(ps[:, g // 4, (g % 4) * P:(g % 4 + 1) * P],
                                                raw[:, g, t * P:(t + 1) * P], id_f[:])
                        last.then_inc(raw_done, 1)
                    t = s - 3
                    if 0 <= t < TT:
                        pe.wait_ge(pick_ready, TT * b + t + 1)
                        pe.matmul(ps[:, 6, E:2 * E], before[:], pick[:], start=True, stop=False)
                        pe.matmul(ps[:, 6, E:2 * E], ones_b[:], taken[:], start=False, stop=True).then_inc(pos_done, 1)
                    t = s - 1
                    if 0 <= t < TT:
                        n = TT * b + t
                        pe.wait_ge(anT_copied, n + 1)
                        if t >= 3:
                            pe.wait_ge(ysh_ready, n - 2)
                        elif t >= 1:
                            pe.wait_ge(un_ready, n)
                        for c in range(DC):
                            last = pe.matmul(ps[:, 3, :], anT[:, c, :], wo_sb[:, c, :], start=c == 0, stop=c == DC - 1)
                        last.then_inc(wo_done, 1)
                    t = s - 3
                    if 0 <= t < TT:
                        n = TT * b + t
                        pe.wait_ge(hid_ready, n + 1)
                        if t + 2 < TT:
                            pe.wait_ge(anT_copied, n + 3)
                        else:
                            pe.wait_ge(hidT_copied, n)
                        for c in range(SIC):
                            last = pe.transpose(ps[:, 2, c * P:(c + 1) * P], hid[:, c * P:(c + 1) * P], id_f[:])
                        last.then_inc(ht_done, 1)
                    t = s - 2
                    if 0 <= t < TT:
                        n = TT * b + t
                        pe.wait_ge(x2T_copied, n + 1)
                        if t >= 1:
                            pe.wait_ge(slot_ready, n)
                        for c in range(DC):
                            last = pe.matmul(ps[:, 6, 0:E], x2T[:, c, :], gw_sb[:, c, :], start=c == 0, stop=c == DC - 1)
                        last.then_inc(rt_done, 1)
                        if t >= 1:
                            pe.wait_ge(hid_ready, n)
                        gu = bank2(2)
                        for c in range(DC):
                            pe.matmul(gu[:, 0:512], x2T[:, c, :], shgu_sb[:, c, 0:512], start=c == 0, stop=c == DC - 1)
                            last = pe.matmul(gu[:, 512:2 * SI], x2T[:, c, :], shgu_sb[:, c, 512:2 * SI],
                                             start=c == 0, stop=c == DC - 1)
                        last.then_inc(gu_done, 1)
                    t = s - 3
                    if 0 <= t < TT:
                        n = TT * b + t
                        pe.wait_ge(hidT_copied, n + 1)
                        if t + 2 < TT:
                            pe.wait_ge(un_ready, n + 3)
                        else:
                            pe.wait_ge(ysh_ready, n)
                        for c in range(SIC):
                            last = pe.matmul(ps[:, 3, :], hidT[:, c, :], shdn_sb[:, c, :], start=c == 0, stop=c == SIC - 1)
                        last.then_inc(dn_done, 1)
                end_phase(pe, b, 2)
            end_late_phase(pe, 0)

            def expert(i, k, skip_first=False, last_one=False):
                e = 4 * i + k
                gu = ps[:, 1 + k % 2, 0:2 * I]

                def half_gate_up(c0):
                    for c in range(c0, c0 + 2):
                        last = pe.matmul(gu, gxT[k % 2][:, c, :], gu_sb[k][:, c, :], start=c == 0, stop=c == DC - 1)
                    return last

                if not last_one:
                    pe.wait_ge(gx_in[(k + 1) % 4], 16 * (i + 1 + (k + 1) // 4))
                    pe.wait_ge(gxT_copied, e + 1)
                    for c in range(DC):
                        last = pe.transpose(ps[:, 0, c * P:(c + 1) * P], gx[(k + 1) % 4][:, c * P:(c + 1) * P], id_f[:])
                    last.then_inc(gxt_done, 1)
                else:
                    pe.wait_ge(gxT_copied, e + 1)
                pe.wait_ge(ew_in[k], 32 * (i + 1))
                half_gate_up(0)
                if not skip_first:
                    hidden_transpose(e - 1, (k - 1) % 2)
                half_gate_up(2).then_inc(egu_done, 1)
                if not skip_first:
                    down(e - 1, (k - 1) % 4)

            def hidden_transpose(e, k2):
                pe.wait_ge(eh_ready, e + 1)
                for c in range(2):
                    last = pe.transpose(ps[0:IH, 3, c * P:(c + 1) * P], eh[k2][:, c * IH:(c + 1) * IH], id_f[:])
                last.then_inc(eht_done, 1)

            def down(e, k):
                pe.wait_ge(ehT_copied, e + 1)
                if not (isinstance(e, int) and e < 2):
                    pe.wait_ge(eo_ready, e - 1)
                for c in range(2):
                    last = pe.matmul(ps[:, 4 + k % 2, :], ehT[k % 2][:, c, :], dn_sb[k][:, c, :], start=c == 0, stop=c == 1)
                last.then_inc(edn_done, 1)

            pe.wait_ge(gx_in[0], 16)
            for c in range(DC):
                last = pe.transpose(ps[:, 0, c * P:(c + 1) * P], gx[0][:, c * P:(c + 1) * P], id_f[:])
            last.then_inc(gxt_done, 1)
            expert(0, 0, skip_first=True)
            for k in range(1, 4):
                expert(0, k)
            with pe.Fori(1, E // 4 - 1) as i:
                for k in range(4):
                    expert(i, k)
            for k in range(4):
                expert(E // 4 - 1, k, last_one=k == 3)
            hidden_transpose(E - 1, 1)
            down(E - 1, 3)
            end_late_phase(pe, 1)

        @block.scalar
        def _(act):
            act.wait_ge(const_ready, 1)
            for rows_past in (acc_d, acc2_d):
                act.dma_start(rows_past[T:T + CAP], blank[:, 0:D]).then_inc(acc_blank, 16)
            act.drain().then_inc(pv_copied, 1)
            for k in range(2):
                act.sem_inc(x1_out[k], 16)
                act.sem_inc(ysh_out[k], 16)
            act.sem_inc(rows_sent, 1)
            with act.Fori(0, NB) as b:
                def copy_xT(t):
                    act.wait_ge(xt_done, TT * b + t + 1)
                    act.activation(xT[t % 2][:].rearrange("p c j -> p (c j)"), ps[:, 6, :], ACT.Copy).then_inc(xt_copied, 1)

                def copy_stack(t, j):
                    n = TT * b + t
                    act.wait_ge(stack_done, 5 * n + j + 1)
                    src = psb[4 + (5 * t + j) % 2][0:QROWS, :].rearrange("p (h j) -> p h j", j=P)
                    dst = (qT[0:QROWS, t // QPH, 8 * j:8 * j + 8, t % QPH * P:(t % QPH + 1) * P] if j < 4 else kT[0:QROWS, :, t * P:(t + 1) * P])
                    act.activation(dst, src, ACT.Copy).then_inc(stack_copied, 1)

                def middle(t):
                    act.wait_ge(rest_ready, TT * b + t + 1)
                    act.activation(stk[t % 2][:, :, 4 * HD:5 * HD], rest[:], ACT.Copy).then_inc(mid_ready, 1)

                def copy_maxT(g, half, bank):
                    gg = KVH * b + g
                    act.wait_ge(maxT_done, 2 * gg + half + 1)
                    act.activation(mT[half][:], psb[bank][0:32, 0:P], ACT.Copy).then_inc(maxT_copied, 1)

                copy_xT(0)
                for s in range(TT + 2):
                    if s == 2:
                        act.wait_ge(rows_sent, b + 1)
                        for k in range(2):
                            act.wait_ge(x1_out[k], 16 * (TT // 2 * b + 1))
                            act.wait_ge(ysh_out[k], 16 * (TT // 2 * b + 1))
                    if s == TT + 1:
                        copy_maxT(0, 0, 7)
                    if s == 4:
                        with act.If(b < 1):
                            act.dma_start(wo_sb[:], w_o.rearrange("(c p) n -> p c n", p=P)).then_inc(late_weights_in, 16)
                            act.dma_start(gw_sb[:], gate_w.rearrange("(c p) n -> p c n", p=P)).then_inc(late_weights_in, 16)
                            act.dma_start(shgu_sb[:], sh_gu.rearrange("(c p) n -> p c n", p=P)).then_inc(late_weights_in, 16)
                            act.dma_start(shdn_sb[:], sh_dn.rearrange("(c p) n -> p c n", p=P)).then_inc(late_weights_in, 16)
                    if s >= 2:
                        copy_stack(s - 2, 0)
                        copy_stack(s - 2, 1)
                    if 1 <= s <= TT:
                        middle(s - 1)
                    if s >= 2:
                        copy_stack(s - 2, 2)
                        copy_stack(s - 2, 3)
                    if s + 1 < TT:
                        copy_xT(s + 1)
                    if s >= 2:
                        copy_stack(s - 2, 4)

                end_phase(act, b, 0)


                def copy_outputs(g, half):
                    gg = KVH * b + g
                    act.wait_ge(pv_done, NP * gg + (HALF1 if half == 0 else NP))
                    act.activation(raw[:, bass.ds(g, 1), half * HALF:(half + 1) * HALF].squeeze(1),
                                   ps[:, 6, :], ACT.Copy).then_inc(pv_copied, 1)

                def group(g, with_next):
                    gg = KVH * b + g
                    for i, (qh, kt, c0) in enumerate(PUNITS):
                        for pair in range(2):
                            act.wait_ge(st_done, 2 * NP * gg + 2 * i + pair + 1)
                            if i >= SLOTS and pair == 0:
                                act.wait_ge(pv_done, NP * gg + i - SLOTS + 1)
                            act.activation(pr[i % SLOTS][:, 2 * pair:2 * pair + 2, 0:HALF - c0],
                                           ps[:, 2 + 2 * pair:4 + 2 * pair, 0:HALF - c0], ACT.Exp,
                                           scale=HD ** -0.5).then_inc(exp_done, 1)
                        if i == T1_STEP:
                            copy_maxT(g, 1, BANK_OF["second"])
                        if i == HALF1 + LAG - 1:
                            copy_outputs(g, 0)
                        if i == T0_STEP and with_next:
                            copy_maxT(g + 1, 0, BANK_OF["first"])
                    copy_outputs(g, 1)

                with act.Fori(0, KVH - 1) as g:
                    group(g, True)
                group(KVH - 1, False)
                end_phase(act, b, 1)

                for s in range(TT + 3):
                    t = s - 1
                    if 0 <= t < TT:
                        act.wait_ge(t1_done, TT * b + t + 1)
                        if t >= 1:
                            act.wait_ge(wo_done, TT * b + t)
                        act.activation(anT[:].rearrange("p c j -> p (c j)"), ps[:, 2, :], ACT.Copy).then_inc(anT_copied, 1)
                    t = s - 2
                    if 0 <= t < TT:
                        act.wait_ge(x2t_done, TT * b + t + 1)
                        if t >= 1:
                            act.wait_ge(gu_done, TT * b + t)
                        act.activation(x2T[:].rearrange("p c j -> p (c j)"), ps[:, 7, :], ACT.Copy).then_inc(x2T_copied, 1)
                    t = s - 3
                    if 0 <= t < TT:
                        act.wait_ge(ht_done, TT * b + t + 1)
                        if t >= 1:
                            act.wait_ge(dn_done, TT * b + t)
                        act.activation(hidT[:].rearrange("p c j -> p (c j)"), ps[:, 2, 0:SI], ACT.Copy).then_inc(hidT_copied, 1)
                    t = s - 2
                    if 0 <= t < TT:
                        n = TT * b + t
                        act.wait_ge(nmax_ready, n + 1)
                        act.activation(pexp[:], ps[:, 6, 0:E], ACT.Exp, bias=nmax[:], accum_out=esum[:]).then_inc(pexp_ready, 1)
                        act.wait_ge(gu_done, n + 1)
                        if t >= 1:
                            act.wait_ge(hid_ready, n)
                        act.activation(sgm[:], ps[:, 4, 0:SI], ACT.Silu).then_inc(sgm_ready, 1)
                    t = s - 3
                    if 0 <= t < TT:
                        n = TT * b + t
                        act.wait_ge(dn_done, n + 1)
                        if t >= 2:
                            act.wait_ge(ysh_out[t % 2], 16 * (TT // 2 * b + t // 2 + 1))
                        act.activation(ysh[t % 2][:], ps[:, 3, :], ACT.Copy).then_inc(ysh_ready, 1)
                end_phase(act, b, 2)
            end_late_phase(act, 0)

            def copy_rowsT(e, k):
                act.wait_ge(gxt_done, e + 1)
                act.activation(gxT[k % 2][:].rearrange("p c j -> p (c j)"), ps[:, 0, :], ACT.Copy).then_inc(gxT_copied, 1)

            def expert(e, k, skip_first=False, last_one=False):
                if not last_one:
                    copy_rowsT(e + 1, k + 1)
                if not skip_first:
                    hiddenT(e - 1, k - 1)
                act.wait_ge(egu_done, e + 1)
                if not skip_first:
                    act.wait_ge(eh_ready, e)
                act.activation(esg[:], ps[:, 1 + k % 2, 0:I], ACT.Silu).then_inc(esg_ready, 1)

            def hiddenT(e, k):
                act.wait_ge(eht_done, e + 1)
                act.activation(ehT[k % 2][:].rearrange("p c j -> p (c j)"), ps[0:IH, 3, 0:2 * P], ACT.Copy).then_inc(ehT_copied, 1)

            copy_rowsT(0, 0)
            expert(0, 0, skip_first=True)
            for k in range(1, 4):
                expert(k, k)
            with act.Fori(1, E // 4 - 1) as i:
                for k in range(4):
                    expert(4 * i + k, k)
            for k in range(4):
                expert(E - 4 + k, k, last_one=k == 3)
            hiddenT(E - 1, 1)
            end_late_phase(act, 1)

        @block.vector
        def _(dve):
            dve.wait_ge(const_ready, 1)
            dve.memset(taken[:], 0.0)
            dve.memset(kT[QROWS:P, :, :], 1.0)
            dve.drain()
            dve.wait_ge(weights_in, 16 * 3)

            def stats(b, t):
                n = TT * b + t
                k = t % 2
                dve.wait_ge(x_in[k], 16 * ((TT // 2) * b + t // 2 + 1))
                dve.bn_stats(st6[:, k, :], xin[k][:])
                dve.drain()
                dve.bn_aggr(mv[:, k, :], st6[:, k, :])
                dve.drain()
                dve.tensor_scalar(vr[:, k:k + 1], mv[:, k, 1:2], EPS, None, ALU.add).then_inc(var_ready, 1)

            def normalise(b, t):
                n = TT * b + t
                k = t % 2
                dve.wait_ge(rstd_ready, n + 1)
                if t >= 2:
                    dve.wait_ge(xt_done, n - 1)
                dve.tensor_scalar(xn[k][:], xin[k][:], mv[:, k, 0:1], rstd[:, k:k + 1],
                                  ALU.subtract, ALU.mult).then_inc(xn_ready, 1)

            for t in range(2):
                stats(0, t)
                normalise(0, t)
            with dve.Fori(0, NB) as b:
                def rotate(t):
                    n = TT * b + t
                    k = t % 2
                    dve.wait_ge(qkv_done, n + 1)
                    acc = ps[:, 2 * k:2 * k + 2, :].rearrange("p a n -> p (a n)")
                    qk = acc[:, 0:NQK].rearrange("p (h d) -> p h d", d=HD)
                    qk2 = acc[:, 0:NQK].rearrange("p (h d two) -> p h d two", d=HD // 2, two=2)
                    cos = ropec_sb[:, t, :].unsqueeze(1).broadcast_to((P, NROT, HD))
                    sn = ropes_sb[:, t, 0:HD // 2].unsqueeze(1).broadcast_to((P, NROT, HD // 2))
                    sp_ = ropes_sb[:, t, HD // 2:HD].unsqueeze(1).broadcast_to((P, NROT, HD // 2))
                    rb2 = rot_b[:].rearrange("p h (d two) -> p h d two", two=2)
                    dve.tensor_tensor(rot_a[:], qk, cos, ALU.mult)
                    dve.tensor_tensor(rb2[:, :, :, 0], qk2[:, :, :, 1], sn, ALU.mult)
                    dve.tensor_tensor(rb2[:, :, :, 1], qk2[:, :, :, 0], sp_, ALU.mult)
                    dve.tensor_copy(v_all[:, t, :, :], acc[:, NQK:NQKV].rearrange("p (h d) -> p h d", d=HD)).then_inc(qkv_read, 1)
                    dve.drain()
                    if t >= 2:
                        dve.wait_ge(low_ready, n - 1)
                        dve.wait_ge(stack_done, 5 * (n - 1))
                    dve.tensor_tensor(rot[k][:], rot_a[:], rot_b[:], ALU.add)
                    dve.drain()
                    dve.tensor_copy(stk[k][:, :, 0:HD], rot[k][:]).then_inc(high_ready, 1)
                    dve.drain()
                    first = stk[k][:, 0:H, 0:HD]
                    dve.tensor_copy(stk[k][:, 0:H, HD:2 * HD], first)
                    dve.tensor_copy(stk[k][:, 0:H, 2 * HD:3 * HD], first)
                    firstk = stk[k][:, H:NROT, 0:HD]
                    dve.tensor_copy(stk[k][:, H:NROT, 3 * HD:4 * HD], firstk)
                    dve.tensor_copy(stk[k][:, H:NROT, 5 * HD:6 * HD], firstk)

                def repeat_middle(t):
                    n = TT * b + t
                    k = t % 2
                    dve.wait_ge(mid_ready, n + 1)
                    dve.tensor_copy(stk[k][:, 0:H, 3 * HD:4 * HD], stk[k][:, 0:H, 4 * HD:5 * HD])
                    dve.tensor_copy(stk[k][:, H:NROT, HD:2 * HD], stk[k][:, H:NROT, 4 * HD:5 * HD]).then_inc(repeats_ready, 1)

                def reduce_unit(g, u, bank, k):
                    half, q, kh, w, heads = UNITS[u]
                    dve.wait_ge(sc_done, NU * (KVH * b + g) + k + 1)
                    n = len(heads)
                    base = 16 * (half + kh)
                    dst = rmax[:, base:base + 16].rearrange("p (h q) -> p h q", q=QPH)
                    dve.tensor_reduce(dst[:, heads[0]:heads[0] + n, q % QPH],
                                      ps[:, bank, 0:n * w].rearrange("p (h k) -> p h k", k=w),
                                      AX, ALU.max).then_inc(sc_reduced, 1)

                def finish_half(g, half):
                    gg = KVH * b + g
                    dve.drain()
                    m = rmax[:, 16 * half:16 * half + 16]
                    if half == 1:
                        dve.tensor_tensor(m, m, rmax[:, 32:48], ALU.max)
                        dve.drain()
                    if not isinstance(g, int):
                        dve.wait_ge(maxT_done, 2 * gg + half - 1)
                    dve.tensor_scalar(mb[half][:, 0:16], m, -1.0, None, ALU.mult)
                    dve.drain()
                    dve.scalar_tensor_tensor(mb[half][:, 16:32], m, -1.0, mb[half][:, 0:16],
                                             ALU.mult, ALU.subtract).then_inc(max_ready, 1)

                for s in range(TT + 2):
                    if 1 <= s and s + 1 < TT:
                        normalise(b, s + 1)
                    if 1 <= s <= TT:
                        rotate(s - 1)
                    if s + 2 < TT:
                        stats(b, s + 2)
                    for k in range(NU):
                        if EARLY_STEP[EARLY[k]] == s:
                            reduce_unit(0, EARLY[k], EARLY_BANK[EARLY[k]], k)
                            if k == NU0 - 1:
                                finish_half(0, 0)
                    if 1 <= s <= TT:
                        repeat_middle(s - 1)
                finish_half(0, 1)
                end_phase(dve, b, 0)

                def maxima(g):
                    for u in range(NU):
                        reduce_unit(g, u, BANK_OF[u], u)
                        if u == NU0 - 1:
                            finish_half(g, 0)
                    finish_half(g, 1)

                with dve.Fori(0, KVH - 1) as g:
                    maxima(g + 1)
                end_phase(dve, b, 1)

                def layer_stats(src, t, j, inc):
                    dve.bn_stats(cst6[:, j, :], src)
                    dve.drain()
                    dve.bn_aggr(cmv[:, j, :], cst6[:, j, :])
                    dve.drain()
                    dve.tensor_scalar(cvr[:, j:j + 1], cmv[:, j, 1:2], EPS, None, ALU.add).then_inc(inc, 1)

                for s in range(TT + 3):
                    t = s
                    if t < TT:
                        n = TT * b + t
                        dve.wait_ge(raw_done, n + 1)
                        rows = ps[:, 0:2, :].rearrange("p a (h d) -> p (a h) d", d=32)
                        dve.reciprocal(rden[:], rows[:, :, HD])
                        dve.drain()
                        if t >= 2:
                            dve.wait_ge(t1_done, n - 1)
                        dve.tensor_tensor(an[t % 2][:], rows[:, :, 0:HD],
                                          rden[:].unsqueeze(2).broadcast_to((P, H, HD)), ALU.mult).then_inc(an_ready, 1)
                    t = s - 3
                    if 0 <= t < TT:
                        n = TT * b + t
                        dve.wait_ge(pos_done, n + 1)
                        dve.tensor_tensor(ohpos[:], onehot[:], ps[:, 6, E:2 * E].unsqueeze(1).broadcast_to((P, TOPK, E)), ALU.mult)
                        dve.tensor_tensor(taken[:], taken[:], pick[:], ALU.add)
                        dve.drain()
                        dve.tensor_reduce(posk[:], ohpos[:], AX, ALU.add)
                        dve.drain()
                        dve.tensor_scalar(over[:], posk[:], float(CAP), float(E * CAP), ALU.is_ge, ALU.mult)
                        dve.scalar_tensor_tensor(slotf[:], idxf[:], float(CAP), posk[:], ALU.mult, ALU.add)
                        dve.drain()
                        dve.tensor_tensor(slot_i[:, t % 4, :], slotf[:], over[:], ALU.add).then_inc(slot_ready, 1)
                    t = s - 1
                    if 0 <= t < TT:
                        n = TT * b + t
                        dve.wait_ge(wo_done, n + 1)
                        layer_stats(ps[:, 3, :], t, 0, cvar_ready)
                        dve.wait_ge(crs_ready, 2 * n + 1)
                        if t >= 1:
                            dve.wait_ge(x1_ready, n)
                        dve.tensor_scalar(un[:], ps[:, 3, :], cmv[:, 0, 0:1], crs[:, 0:1],
                                          ALU.subtract, ALU.mult).then_inc(un_ready, 1)
                    t = s - 2
                    if 0 <= t < TT:
                        n = TT * b + t
                        dve.wait_ge(rt_done, n + 1)
                        if t >= 1:
                            dve.wait_ge(pexp_ready, n)
                        dve.tensor_reduce(nmax[:], ps[:, 6, 0:E], AX, ALU.max, negate=True).then_inc(nmax_ready, 1)
                    t = s - 1
                    if 0 <= t < TT:
                        n = TT * b + t
                        dve.wait_ge(x1_ready, n + 1)
                        layer_stats(x1[t % 2][:], t, 1, cvar_ready)
                    t = s - 2
                    if 0 <= t < TT:
                        n = TT * b + t
                        sc = x2[t % 4][:, D:D + E]
                        dve.wait_ge(pexp_ready, n + 1)
                        dve.reciprocal(rsum[:], esum[:])
                        dve.drain()
                        dve.tensor_scalar(sc, pexp[:], rsum[:], None, ALU.mult)
                        dve.drain()
                        dve.max(top8[:], sc)
                        dve.drain()
                        dve.max_index(idx8[:], top8[:], sc)
                        dve.drain()
                        dve.tensor_copy(idxf[:], idx8[:, 0:TOPK])
                        dve.drain()
                        dve.tensor_tensor(onehot[:], iota_e[:].unsqueeze(1).broadcast_to((P, TOPK, E)),
                                          idxf[:].unsqueeze(2).broadcast_to((P, TOPK, E)), ALU.is_equal)
                        dve.drain()
                        with nc.allow_low_precision("a sum of zeros and at most one 1"):
                            dve.tensor_reduce(pick[:], onehot[:].rearrange("p k e -> p e k"), AX, ALU.add).then_inc(pick_ready, 1)
                    t = s - 1
                    if 0 <= t < TT:
                        n = TT * b + t
                        dve.wait_ge(crs_ready, 2 * n + 2)
                        if t >= 4:
                            dve.wait_ge(sent[t % 4], 16 * TOPK * (TT // 4 * b + t // 4))
                        dve.tensor_copy(x2[t % 4][:, TOKCOL:TOKCOL + 1].bitcast(i32), tok[:])
                        dve.tensor_scalar(x2[t % 4][:, 0:D], x1[t % 2][:], cmv[:, 1, 0:1], crs[:, 1:2],
                                          ALU.subtract, ALU.mult).then_inc(x2_ready, 1)
                        dve.tensor_scalar(tok[:], tok[:], float(P), None, ALU.add)
                    t = s - 2
                    if 0 <= t < TT:
                        n = TT * b + t
                        dve.wait_ge(sgm_ready, n + 1)
                        gu = ps[:, 4:6, :].rearrange("p a n -> p (a n)")
                        if t >= 1:
                            dve.wait_ge(ht_done, n)
                        dve.tensor_tensor(hid[:], gu[:, SI:2 * SI], sgm[:], ALU.mult).then_inc(hid_ready, 1)
                    if s == TT + 1:
                        with dve.If(b < NB - 1):
                            for t in range(2):
                                stats(b + 1, t)
                                normalise(b + 1, t)
                end_phase(dve, b, 2)
            end_late_phase(dve, 0)

            def gated(e, k):
                dve.wait_ge(esg_ready, e + 1)
                gu = ps[:, 1 + k % 2, :]
                dve.tensor_tensor(eh[k % 2][:], gu[:, I:2 * I], esg[:], ALU.mult).then_inc(eh_ready, 1)

            def scaled_at(i, k, first=False):
                e = 4 * i + k
                dve.wait_ge(edn_done, e + 1)
                if not first:
                    dve.wait_ge(added[k % 2], 16 * (2 * i + k // 2 - 1))
                dve.tensor_copy(etok[k][:], gx[k][:, TOKCOL:TOKCOL + 1].bitcast(i32))
                dve.tensor_scalar(eo[k][:], ps[:, 4 + k % 2, :], gx[k][:, bass.ds(D + e, 1)], None,
                                  ALU.mult).then_inc(eo_ready, 1)

            gated(0, 0)
            for k in range(1, 4):
                gated(k, k)
                scaled_at(0, k - 1, first=True)
            gated(4, 0)
            scaled_at(0, 3, first=True)
            for k in range(1, 4):
                gated(4 + k, k)
                scaled_at(1, k - 1)
            with dve.Fori(2, E // 4) as i:
                for k in range(4):
                    gated(4 * i + k, k)
                    if k == 0:
                        scaled_at(i - 1, 3)
                    else:
                        scaled_at(i, k - 1)
            scaled_at(E // 4 - 1, 3)
            end_late_phase(dve, 1)

            fin = T // (P * FT)

            def f_stats(j):
                k = j % 2
                fb = fy[j % FB]
                dve.wait_ge(f_in[j % FB], 32 * (j // FB + 1))
                dve.tensor_tensor(fb[:], fb[:], fz[j % FB][:], ALU.add)
                dve.drain()
                for f in range(FT):
                    dve.bn_stats(fst[:, k, f, :], fb[:, f, :])
                dve.drain()
                for f in range(FT):
                    dve.bn_aggr(fmv[:, k, f, :], fst[:, k, f, :])
                dve.drain()
                dve.tensor_scalar(fvr[:, k, :], fmv[:, k, :, 1], EPS, None, ALU.add).then_inc(fvar_ready, 1)

            f_stats(0)
            for j in range(fin):
                k = j % 2
                if j + 1 < fin:
                    f_stats(j + 1)
                dve.wait_ge(frs_ready, j + 1)
                for f in range(FT):
                    last = dve.tensor_scalar(fy[j % FB][:, f, :], fy[j % FB][:, f, :], fmv[:, k, f, 0:1], frs[:, k, f:f + 1],
                                             ALU.subtract, ALU.mult)
                last.then_inc(fn_ready, 1)

        @block.gpsimd
        def _(pool):
            for m in (id_b, id_f):
                pool.memset(m[:], 0.0)
            pool.memset(minus_half[:], -0.5)
            pool.memset(causal[:], 0.0)
            pool.memset(before[:], 0.0)
            pool.memset(ones_b[:], 1.0)
            pool.memset(v_ones[:], 1.0)
            pool.memset(blank[:], 0.0)
            pool.iota(tok[:], pattern=[[0, 1]], base=0, channel_multiplier=1, allow_small_or_imprecise_dtypes=True)
            pool.iota(iota_e[:], pattern=[[1, E]], base=0, channel_multiplier=0, allow_small_or_imprecise_dtypes=True)
            pool.drain()
            for m in (id_b, id_f):
                pool.affine_select(out=m[:], in_=m[:], compare_op=ALU.not_equal, fill=1.0, base=0,
                                   pattern=[[-1, P]], channel_multiplier=1)
            pool.affine_select(out=causal[:], in_=causal[:], compare_op=ALU.is_ge, fill=NEG, base=0,
                               pattern=[[-1, P]], channel_multiplier=1)
            pool.affine_select(out=before[:], in_=before[:], compare_op=ALU.is_ge, fill=1.0, base=0,
                               pattern=[[-1, P]], channel_multiplier=1)
            pool.iota(blank[:, TOKCOL:TOKCOL + 1].bitcast(i32), pattern=[[0, 1]], base=T, channel_multiplier=1)
            pool.drain().then_inc(const_ready, 1)

            def power(b, t):
                n = TT * b + t
                k = t % 2
                pool.wait_ge(var_ready, n + 1)
                pool.tensor_tensor(rstd[:, k:k + 1], vr[:, k:k + 1], minus_half[:, 0:1], ALU.pow).then_inc(rstd_ready, 1)

            power(0, 0)
            power(0, 1)
            with pool.Fori(0, NB) as b:
                def pieces(t):
                    n = TT * b + t
                    k = t % 2
                    pool.wait_ge(high_ready, n + 1)
                    if t >= 1:
                        pool.wait_ge(low_ready, n)
                    pool.tensor_tensor(rest[:], rot[k][:], stk[k][:, :, 0:HD], ALU.subtract).then_inc(rest_ready, 1)
                    pool.wait_ge(mid_ready, n + 1)
                    pool.tensor_tensor(stk[k][:, 0:H, 5 * HD:6 * HD], rest[:, 0:H, :], stk[k][:, 0:H, 4 * HD:5 * HD], ALU.subtract)
                    pool.tensor_tensor(stk[k][:, H:NROT, 2 * HD:3 * HD], rest[:, H:NROT, :],
                                       stk[k][:, H:NROT, 4 * HD:5 * HD], ALU.subtract).then_inc(low_ready, 1)

                for s in range(TT + 1):
                    if s >= 1:
                        pieces(s - 1)
                    if s + 2 < TT:
                        power(b, s + 2)
                end_phase(pool, b, 0)

                def copy_v(g):
                    pool.tensor_copy(v_ones[:, :, 0:HD], v_all[:, :, bass.ds(g, 1), :].squeeze(2)).then_inc(v_ready, 1)

                def group(g, with_next):
                    gg = KVH * b + g
                    d = 0
                    for i, (qh, kt, c0) in enumerate(PUNITS):
                        if DIAG[i]:
                            wait_apart(pool, exp_done, 2 * NP * gg + 2 * i + 2)
                            tile = pr[i % SLOTS][:, :, 0:P]
                            pool.affine_select(out=tile, in_=tile, compare_op=ALU.is_ge, fill=0.0, base=0,
                                               pattern=[[0, REP], [1, P]], channel_multiplier=-1).then_inc(masked, 1)
                            d += 1
                    if with_next:
                        wait_apart(pool, pv_done, NP * (gg + 1))
                        copy_v(g + 1)

                copy_v(0)
                with pool.Fori(0, KVH - 1) as g:
                    group(g, True)
                group(KVH - 1, False)
                end_phase(pool, b, 1)

                pool.wait_ge(disp_blank, 16 * KVH)
                for s in range(TT + 3):
                    t = s - 1
                    if 0 <= t < TT:
                        n = TT * b + t
                        k = t % 2
                        pool.wait_ge(cvar_ready, 2 * n + 1)
                        pool.tensor_tensor(crs[:, 0:1], cvr[:, 0:1], minus_half[:, 0:1], ALU.pow).then_inc(crs_ready, 1)
                        pool.wait_ge(un_ready, n + 1)
                        pool.wait_ge(xres_in[k], 16 * ((TT // 2) * b + t // 2 + 1))
                        if t >= 2:
                            pool.wait_ge(x1_out[k], 16 * (TT // 2 * b + t // 2 + 1))
                            pool.wait_ge(x2_ready, n - 1)
                        pool.tensor_tensor(x1[k][:], un[:], xres[k][:], ALU.add).then_inc(x1_ready, 1)
                        pool.wait_ge(cvar_ready, 2 * n + 2)
                        pool.tensor_tensor(crs[:, 1:2], cvr[:, 1:2], minus_half[:, 0:1], ALU.pow).then_inc(crs_ready, 1)
                    t = s - 3
                    if t == TT - 1:
                        wait_apart(pool, x1_ready, TT * (b + 1))
                        wait_apart(pool, crs_ready, 2 * TT * (b + 1))
                        with pool.If(b < NB - 1):
                            wait_apart(pool, rstd_ready, TT * (b + 1) + 2)
                        pool.sem_inc(phase_end, 1)
                    if 0 <= t < TT:
                        n = TT * b + t
                        wait_apart(pool, slot_ready, n + 1)
                        for k in range(TOPK):
                            pool.indirect_dma_start(
                                out=disp_d, out_offset=bass.IndirectOffsetOnAxis(ap=slot_i[:, t % 4, k:k + 1], axis=0),
                                in_=x2[t % 4][:], in_offset=None, bounds_check=E * CAP - 1,
                                oob_is_err=False).then_inc(sent[t % 4], 16)
                    if s == TT + 1:
                        with pool.If(b < NB - 1):
                            power(b + 1, 0)
                            power(b + 1, 1)
                for k in range(4):
                    wait_apart(pool, sent[k], 16 * TOPK * (TT // 4) * (b + 1))
                pool.sem_inc(rows_sent, 1)
                wait_apart(pool, phase_end, (b * PHASES + 3) * ENGINES)
            end_late_phase(pool, 0)

            def add_rows(e, k):
                wait_apart(pool, eo_ready, e + 1)
                pool.indirect_dma_start(
                    out=(acc_d, acc2_d)[k % 2], out_offset=bass.IndirectOffsetOnAxis(ap=etok[k][:], axis=0),
                    in_=eo[k][:], in_offset=None, bounds_check=T + CAP - 1, compute_op=ALU.add).then_inc(added[k % 2], 16)

            pool.wait_ge(acc_blank, 16 * (2 + NT))
            for k in range(4):
                if k >= 2:
                    pool.wait_ge(added[k % 2], 16)
                add_rows(k, k)
            with pool.Fori(1, E // 4) as i:
                for k in range(4):
                    pool.wait_ge(added[k % 2], 16 * (2 * i + k // 2))
                    add_rows(4 * i + k, k)
            for k in range(2):
                pool.wait_ge(added[k], 16 * E // 2)
            end_late_phase(pool, 1)

            def f_sum(j):
                k = j % FB
                pool.wait_ge(fn_ready, j + 1)
                pool.tensor_tensor(fz[k][:], fy[k][:], x1_all[:, FT * j:FT * (j + 1), :], ALU.add).then_inc(fo_ready, 1)

            for j in range(T // (P * FT)):
                k = j % 2
                pool.wait_ge(fvar_ready, j + 1)
                pool.tensor_tensor(frs[:, k, :], fvr[:, k, :], minus_half[:, 0:FT], ALU.pow).then_inc(frs_ready, 1)
                if j:
                    f_sum(j - 1)
            f_sum(T // (P * FT) - 1)


def rope_tables():
    half = HD // 2
    inv = (np.float32(1) / np.float32(10000) ** (np.arange(half, dtype=np.float32) / np.float32(half))).astype(np.float32)
    ang = np.outer(np.arange(S, dtype=np.float32), inv)
    c, s = np.cos(ang), np.sin(ang)
    return np.repeat(c, 2, axis=1).astype(np.float32), np.concatenate([-s, s], axis=1).astype(np.float32)


def kernel(**inputs):
    import concourse.bacc as bacc
    from concourse.bass_utils import run_bass_kernel_spmd as run

    a = {k: np.asarray(v) for k, v in inputs.items()}
    c, s = rope_tables()
    arrays = {
        "x": a["L0_attn_x"].reshape(T, D),
        "w_qkv": np.concatenate([a["L0_attn_Wq"], a["L0_attn_Wk"], a["L0_attn_Wv"]], axis=1),
        "w_o": a["L0_attn_Wo"],
        "gate_w": np.ascontiguousarray(a["L0_ffn_gate_w"].T),
        "w_gu": a["L0_ffn_gate_up_proj"],
        "w_dn": a["L0_ffn_down_proj"],
        "sh_gu": np.ascontiguousarray(np.concatenate([a["L0_ffn_shared_gate_w"], a["L0_ffn_shared_up_w"]], axis=0).T),
        "sh_dn": np.ascontiguousarray(a["L0_ffn_shared_down_w"].T),
        "rope_c": c,
        "rope_s": s,
    }
    f32 = mybir.dt.float32
    nc = bacc.Bacc("TRN2", target_bir_lowering=False, num_devices=1)
    args = [nc.dram_tensor(f"{k}_dram", v.shape, f32, kind="ExternalInput").ap() for k, v in arrays.items()]
    out = nc.dram_tensor("out_dram", (T, D), f32, kind="ExternalOutput").ap()
    x1_d = nc.dram_tensor("x1_scratch", (T, D), f32, kind="Internal").ap()
    acc_d = nc.dram_tensor("acc_scratch", (T + CAP, D), f32, kind="Internal").ap()
    acc2_d = nc.dram_tensor("acc2_scratch", (T + CAP, D), f32, kind="Internal").ap()
    disp_d = nc.dram_tensor("dispatch_scratch", (E * CAP, ROW), f32, kind="Internal").ap()
    program(nc, *args, out, x1_d, acc_d, acc2_d, disp_d)
    r = run(nc, [{f"{k}_dram": v for k, v in arrays.items()}], core_ids=[0])
    return r.results[0]["out_dram"].reshape(NB, S, D)
```
